# Optimizing a Trainium2 kernel written in Bass

```python
import numpy as np
import jax
import jax.numpy as jnp

def _softmax(x, axis=-1):
    return jax.nn.softmax(x, axis=axis)
def _gelu(x):
    return jax.nn.gelu(x, approximate=True)
def _silu(x):
    return jax.nn.silu(x)
def _sigmoid(x):
    return jax.nn.sigmoid(x)
def _layernorm(x, axis=-1, eps=1e-5):
    m = jnp.mean(x, axis=axis, keepdims=True)
    v = jnp.var(x, axis=axis, keepdims=True)
    return (x - m) / jnp.sqrt(v + eps)
def _scatter_add(tgt, idx, src, axis=0):
    return tgt.at[idx].add(src)
def _segment_sum(src, seg, n):
    return jax.ops.segment_sum(src, seg, n)

kernel_name = 'mk_conv_preact_d2_conv_nchw512_8e5964'

def setup_inputs(seed: int = 0):
    np.random.seed(seed)
    _w = jnp.asarray
    def _rec_inputs():
        import jax
        import jax.numpy as jnp
        _gk = jax.random.key(seed)
        x = -0.0002928 + 1 * jax.random.normal(jax.random.fold_in(_gk, 1), (2, 512, 64, 64), jnp.float32)
        return x
    x = _rec_inputs()
    def _L0_conv_setup():
        import jax, jax.numpy as jnp
        import numpy as np
        C = 512
        G = 16
        Cg = C // G
        K = 3
        P = K * K
        PAD = 1
        STRIDE = 1
        DIL = 1
        DWK = 3
        OFFSET_SCALE = 1.0
        LN_EPS = 1e-05

        def _dcnv3_core(x, offset, mask):
            N, H, W, _ = x.shape
            Hin, Win = (H + 2 * PAD, W + 2 * PAD)
            Hout, Wout = (H, W)
            xpad = jnp.pad(x, ((0, 0), (PAD, PAD), (PAD, PAD), (0, 0)))
            base = DIL * (K - 1) // 2 + 0.5
            ref_y = (base + jnp.arange(Hout, dtype=jnp.float32) * STRIDE) / Hin
            ref_x = (base + jnp.arange(Wout, dtype=jnp.float32) * STRIDE) / Win
            ref = jnp.stack(jnp.broadcast_arrays(ref_x[None, :], ref_y[:, None]), -1)
            g1 = jnp.arange(K, dtype=jnp.float32) * DIL - DIL * (K - 1) // 2
            gxx, gyy = jnp.meshgrid(g1 / Win, g1 / Hin, indexing='ij')
            grid = jnp.stack([gxx, gyy], -1).reshape(P, 2)
            off = offset.reshape(N, Hout, Wout, G, P, 2)
            norm = jnp.array([Win, Hin], jnp.float32)
            loc = ref[None, :, :, None, None, :] + grid * OFFSET_SCALE + off * OFFSET_SCALE / norm
            px = loc[..., 0] * Win - 0.5
            py = loc[..., 1] * Hin - 0.5
            xg = xpad.reshape(N, Hin, Win, G, Cg).transpose(0, 3, 1, 2, 4).reshape(N * G, Hin, Win, Cg)
            pxg = px.transpose(0, 3, 1, 2, 4).reshape(N * G, Hout, Wout, P)
            pyg = py.transpose(0, 3, 1, 2, 4).reshape(N * G, Hout, Wout, P)
            mg = mask.transpose(0, 3, 1, 2, 4).reshape(N * G, Hout, Wout, P)

            def bilin(img, bx, by, m):
                x0 = jnp.floor(bx)
                y0 = jnp.floor(by)
                wx = (bx - x0)[..., None]
                wy = (by - y0)[..., None]
                x0i = x0.astype(jnp.int32)
                y0i = y0.astype(jnp.int32)

                def g(yy, xx):
                    valid = (yy >= 0) & (yy < Hin) & (xx >= 0) & (xx < Win)
                    v = img[jnp.clip(yy, 0, Hin - 1), jnp.clip(xx, 0, Win - 1)]
                    return v * valid[..., None]
                v00 = g(y0i, x0i)
                v01 = g(y0i, x0i + 1)
                v10 = g(y0i + 1, x0i)
                v11 = g(y0i + 1, x0i + 1)
                samp = (v00 * (1 - wx) + v01 * wx) * (1 - wy) + (v10 * (1 - wx) + v11 * wx) * wy
                return jnp.einsum('hwpc,hwp->hwc', samp, m)
            out = jax.vmap(bilin)(xg, pxg, pyg, mg)
            return out.reshape(N, G, Hout, Wout, Cg).transpose(0, 2, 3, 1, 4).reshape(N, Hout, Wout, C)
        key = jax.random.key(seed)
        ks = jax.random.split(key, 10)
        N, H, W = (2, 64, 64)
        sc = 1.0 / np.sqrt(C)
        return {'x': jax.random.normal(ks[0], (N, C, H, W), jnp.float32), 'dw_w': jax.random.normal(ks[1], (C, 1, DWK, DWK), jnp.float32) * 0.1, 'dw_b': jax.random.normal(ks[2], (C,), jnp.float32) * 0.02, 'ln_g': jnp.ones((C,), jnp.float32), 'ln_b': jnp.zeros((C,), jnp.float32), 'off_w': jax.random.normal(ks[3], (C, G * P * 2), jnp.float32) * 0.01, 'off_b': jax.random.normal(ks[4], (G * P * 2,), jnp.float32) * 0.01, 'mask_w': jax.random.normal(ks[5], (C, G * P), jnp.float32) * 0.01, 'mask_b': jnp.zeros((G * P,), jnp.float32), 'in_w': jax.random.normal(ks[6], (C, C), jnp.float32) * sc, 'in_b': jnp.zeros((C,), jnp.float32), 'out_w': jax.random.normal(ks[7], (C, C), jnp.float32) * sc, 'out_b': jnp.zeros((C,), jnp.float32)}
    _L0_conv_all = _L0_conv_setup()
    _L0_conv_in = {k: v for k, v in _L0_conv_all.items() if k in ('dw_w', 'dw_b', 'ln_g', 'ln_b', 'off_w', 'off_b', 'mask_w', 'mask_b', 'in_w', 'in_b', 'out_w', 'out_b', )}
    del _L0_conv_all

    def _L1_conv_setup():
        import jax, jax.numpy as jnp
        import numpy as np
        from jax import lax
        DN = ('NCHW', 'OIHW', 'NCHW')

        def _conv(x, w, pad):
            return lax.conv_general_dilated(x, w, (1, 1), pad, dimension_numbers=DN)

        def _bn(x, p, eps=1e-05):
            g, b, m, v = (p[0], p[1], p[2], p[3])
            scale = g / jnp.sqrt(v + eps)
            return (x - m[:, None, None]) * scale[:, None, None] + b[:, None, None]
        key = jax.random.key(seed)
        ks = jax.random.split(key, 12)
        B, C, H, W = (16, 512, 56, 56)
        mid = C // 2

        def bn_params(k):
            k1, k2, k3, k4 = jax.random.split(k, 4)
            g = 1.0 + 0.1 * jax.random.normal(k1, (mid,), jnp.float32)
            b = 0.1 * jax.random.normal(k2, (mid,), jnp.float32)
            m = 0.1 * jax.random.normal(k3, (mid,), jnp.float32)
            v = 0.5 + jax.random.uniform(k4, (mid,), jnp.float32)
            return jnp.stack([g, b, m, v])
        return {'x': jax.random.normal(ks[0], (B, C, H, W), jnp.float32), 'w_main': 0.03 * jax.random.normal(ks[1], (mid, C, 3, 3), jnp.float32), 'w_1x1': 0.05 * jax.random.normal(ks[2], (mid, C, 1, 1), jnp.float32), 'w31': 0.05 * jax.random.normal(ks[3], (mid, C, 1, 1), jnp.float32), 'bn31': bn_params(ks[4]), 'w33': 0.05 * jax.random.normal(ks[5], (mid, mid, 3, 3), jnp.float32), 'bn33': bn_params(ks[6]), 'wa1': 0.05 * jax.random.normal(ks[7], (mid, C, 1, 1), jnp.float32), 'bna1': bn_params(ks[8]), 'bna2': bn_params(ks[9]), 'fuse_weight': jnp.ones((4,), jnp.float32), 'c_score': jax.random.normal(ks[10], (2 * C,), jnp.float32)}
    _L1_conv_all = _L1_conv_setup()
    _L1_conv_in = {k: v for k, v in _L1_conv_all.items() if k in ('w_main', 'w_1x1', 'w31', 'bn31', 'w33', 'bn33', 'wa1', 'bna1', 'bna2', 'fuse_weight', 'c_score', )}
    del _L1_conv_all

    return {
        "x": x,
        "L0_conv_dw_w": _L0_conv_in["dw_w"],
        "L0_conv_dw_b": _L0_conv_in["dw_b"],
        "L0_conv_ln_g": _L0_conv_in["ln_g"],
        "L0_conv_ln_b": _L0_conv_in["ln_b"],
        "L0_conv_off_w": _L0_conv_in["off_w"],
        "L0_conv_off_b": _L0_conv_in["off_b"],
        "L0_conv_mask_w": _L0_conv_in["mask_w"],
        "L0_conv_mask_b": _L0_conv_in["mask_b"],
        "L0_conv_in_w": _L0_conv_in["in_w"],
        "L0_conv_in_b": _L0_conv_in["in_b"],
        "L0_conv_out_w": _L0_conv_in["out_w"],
        "L0_conv_out_b": _L0_conv_in["out_b"],
        "L1_conv_w_main": _L1_conv_in["w_main"],
        "L1_conv_w_1x1": _L1_conv_in["w_1x1"],
        "L1_conv_w31": _L1_conv_in["w31"],
        "L1_conv_bn31": _L1_conv_in["bn31"],
        "L1_conv_w33": _L1_conv_in["w33"],
        "L1_conv_bn33": _L1_conv_in["bn33"],
        "L1_conv_wa1": _L1_conv_in["wa1"],
        "L1_conv_bna1": _L1_conv_in["bna1"],
        "L1_conv_bna2": _L1_conv_in["bna2"],
        "L1_conv_fuse_weight": _L1_conv_in["fuse_weight"],
        "L1_conv_c_score": _L1_conv_in["c_score"],
    }

def reference(x, L0_conv_dw_w, L0_conv_dw_b, L0_conv_ln_g, L0_conv_ln_b, L0_conv_off_w, L0_conv_off_b, L0_conv_mask_w, L0_conv_mask_b, L0_conv_in_w, L0_conv_in_b, L0_conv_out_w, L0_conv_out_b, L1_conv_w_main, L1_conv_w_1x1, L1_conv_w31, L1_conv_bn31, L1_conv_w33, L1_conv_bn33, L1_conv_wa1, L1_conv_bna1, L1_conv_bna2, L1_conv_fuse_weight, L1_conv_c_score):
    import jax
    import jax.numpy as jnp
    def _L0_conv_ref(x, dw_w, dw_b, ln_g, ln_b, off_w, off_b, mask_w, mask_b, in_w, in_b, out_w, out_b):
        import jax, jax.numpy as jnp
        import numpy as np
        C = 512
        G = 16
        Cg = C // G
        K = 3
        P = K * K
        PAD = 1
        STRIDE = 1
        DIL = 1
        DWK = 3
        OFFSET_SCALE = 1.0
        LN_EPS = 1e-05

        def _dcnv3_core(x, offset, mask):
            N, H, W, _ = x.shape
            Hin, Win = (H + 2 * PAD, W + 2 * PAD)
            Hout, Wout = (H, W)
            xpad = jnp.pad(x, ((0, 0), (PAD, PAD), (PAD, PAD), (0, 0)))
            base = DIL * (K - 1) // 2 + 0.5
            ref_y = (base + jnp.arange(Hout, dtype=jnp.float32) * STRIDE) / Hin
            ref_x = (base + jnp.arange(Wout, dtype=jnp.float32) * STRIDE) / Win
            ref = jnp.stack(jnp.broadcast_arrays(ref_x[None, :], ref_y[:, None]), -1)
            g1 = jnp.arange(K, dtype=jnp.float32) * DIL - DIL * (K - 1) // 2
            gxx, gyy = jnp.meshgrid(g1 / Win, g1 / Hin, indexing='ij')
            grid = jnp.stack([gxx, gyy], -1).reshape(P, 2)
            off = offset.reshape(N, Hout, Wout, G, P, 2)
            norm = jnp.array([Win, Hin], jnp.float32)
            loc = ref[None, :, :, None, None, :] + grid * OFFSET_SCALE + off * OFFSET_SCALE / norm
            px = loc[..., 0] * Win - 0.5
            py = loc[..., 1] * Hin - 0.5
            xg = xpad.reshape(N, Hin, Win, G, Cg).transpose(0, 3, 1, 2, 4).reshape(N * G, Hin, Win, Cg)
            pxg = px.transpose(0, 3, 1, 2, 4).reshape(N * G, Hout, Wout, P)
            pyg = py.transpose(0, 3, 1, 2, 4).reshape(N * G, Hout, Wout, P)
            mg = mask.transpose(0, 3, 1, 2, 4).reshape(N * G, Hout, Wout, P)

            def bilin(img, bx, by, m):
                x0 = jnp.floor(bx)
                y0 = jnp.floor(by)
                wx = (bx - x0)[..., None]
                wy = (by - y0)[..., None]
                x0i = x0.astype(jnp.int32)
                y0i = y0.astype(jnp.int32)

                def g(yy, xx):
                    valid = (yy >= 0) & (yy < Hin) & (xx >= 0) & (xx < Win)
                    v = img[jnp.clip(yy, 0, Hin - 1), jnp.clip(xx, 0, Win - 1)]
                    return v * valid[..., None]
                v00 = g(y0i, x0i)
                v01 = g(y0i, x0i + 1)
                v10 = g(y0i + 1, x0i)
                v11 = g(y0i + 1, x0i + 1)
                samp = (v00 * (1 - wx) + v01 * wx) * (1 - wy) + (v10 * (1 - wx) + v11 * wx) * wy
                return jnp.einsum('hwpc,hwp->hwc', samp, m)
            out = jax.vmap(bilin)(xg, pxg, pyg, mg)
            return out.reshape(N, G, Hout, Wout, Cg).transpose(0, 2, 3, 1, 4).reshape(N, Hout, Wout, C)
        N, _, H, W = x.shape
        inp = jnp.transpose(x, (0, 2, 3, 1))
        xproj = inp @ in_w + in_b
        x1 = jax.lax.conv_general_dilated(x, dw_w, (1, 1), [((DWK - 1) // 2, (DWK - 1) // 2)] * 2, feature_group_count=C, dimension_numbers=('NCHW', 'OIHW', 'NCHW'))
        x1 = jnp.transpose(x1, (0, 2, 3, 1)) + dw_b
        mu = x1.mean(-1, keepdims=True)
        var = ((x1 - mu) ** 2).mean(-1, keepdims=True)
        x1 = (x1 - mu) / jnp.sqrt(var + LN_EPS) * ln_g + ln_b
        x1 = jax.nn.gelu(x1, approximate=False)
        offset = x1 @ off_w + off_b
        mask = jax.nn.softmax((x1 @ mask_w + mask_b).reshape(N, H, W, G, P), -1)
        out = _dcnv3_core(xproj, offset, mask)
        out = out @ out_w + out_b
        return jnp.transpose(out, (0, 3, 1, 2))

    def _L1_conv_ref(x, w_main, w_1x1, w31, bn31, w33, bn33, wa1, bna1, bna2, fuse_weight, c_score):
        import jax, jax.numpy as jnp
        import numpy as np
        from jax import lax
        DN = ('NCHW', 'OIHW', 'NCHW')

        def _conv(x, w, pad):
            return lax.conv_general_dilated(x, w, (1, 1), pad, dimension_numbers=DN)

        def _bn(x, p, eps=1e-05):
            g, b, m, v = (p[0], p[1], p[2], p[3])
            scale = g / jnp.sqrt(v + eps)
            return (x - m[:, None, None]) * scale[:, None, None] + b[:, None, None]
        c = x.shape[1]
        acs_main = _conv(x * fuse_weight[0], w_main, 'SAME')
        acs_1x1 = _conv(x * fuse_weight[1], w_1x1, 'VALID')
        acs_3x3 = _bn(_conv(_bn(_conv(x * fuse_weight[2], w31, 'VALID'), bn31), w33, 'SAME'), bn33)
        avg_in = _bn(_conv(x * fuse_weight[3], wa1, 'VALID'), bna1)
        pooled = lax.reduce_window(avg_in, 0.0, lax.add, (1, 1, 3, 3), (1, 1, 1, 1), [(0, 0), (0, 0), (1, 1), (1, 1)]) / 9.0
        acs_avg = _bn(pooled, bna2)
        out = jnp.concatenate([acs_main, acs_1x1, acs_3x3, acs_avg], axis=1)
        _, ind = lax.top_k(c_score, c)
        scale = jax.nn.sigmoid(c_score)[ind]
        out = out[:, ind] * scale[None, :, None, None]
        return out

    def _gn(v, G=32, eps=1e-5):
        B_, C_, H_, W_ = v.shape
        g = v.reshape(B_, G, C_ // G, H_, W_)
        m = jnp.mean(g, axis=(2, 3, 4), keepdims=True)
        s = jnp.var(g, axis=(2, 3, 4), keepdims=True)
        return ((g - m) / jnp.sqrt(s + eps)).reshape(v.shape)

    def _ln_c(v, eps=1e-6):
        m = jnp.mean(v, axis=1, keepdims=True)
        s = jnp.var(v, axis=1, keepdims=True)
        return (v - m) / jnp.sqrt(s + eps)

    def _ln_t(v, eps=1e-5):
        m = jnp.mean(v, axis=-1, keepdims=True)
        s = jnp.var(v, axis=-1, keepdims=True)
        return (v - m) / jnp.sqrt(s + eps)

    def _to_tokens(v):
        B_, C_, H_, W_ = v.shape
        return v.reshape(B_, C_, H_ * W_).transpose(0, 2, 1)
    def _from_tokens(t, like):
        B_, C_, H_, W_ = like.shape
        return t.transpose(0, 2, 1).reshape(B_, C_, H_, W_)

    x = x + _L0_conv_ref(_gn(x), L0_conv_dw_w, L0_conv_dw_b, L0_conv_ln_g, L0_conv_ln_b, L0_conv_off_w, L0_conv_off_b, L0_conv_mask_w, L0_conv_mask_b, L0_conv_in_w, L0_conv_in_b, L0_conv_out_w, L0_conv_out_b)
    x = x + _L1_conv_ref(_gn(x), L1_conv_w_main, L1_conv_w_1x1, L1_conv_w31, L1_conv_bn31, L1_conv_w33, L1_conv_bn33, L1_conv_wa1, L1_conv_bna1, L1_conv_bna2, L1_conv_fuse_weight, L1_conv_c_score)
    return x


_drawn_inputs = setup_inputs


def setup_inputs(seed=0):
    import zlib

    import numpy as np

    out = dict(_drawn_inputs(seed))
    spreads = {'L0_conv_ln_g': (1.0, 0.6),
     'L0_conv_ln_b': (0.0, 0.8),
     'L0_conv_in_b': (0.0, 0.1),
     'L0_conv_out_b': (0.0, 0.1),
     'L1_conv_fuse_weight': (1.0, 0.2)}
    factors = {'L0_conv_dw_b': 8.0, 'L0_conv_off_b': 8.0}
    for name, (base, spread) in spreads.items():
        noise = np.random.default_rng([zlib.crc32(name.encode()), seed]).standard_normal(out[name].shape)
        drawn = base * np.exp(spread * noise) if base else spread * noise
        out[name] = jnp.asarray(drawn.astype(out[name].dtype))
    for name, factor in factors.items():
        out[name] = (out[name] * factor).astype(out[name].dtype)
    return out
```

```python
from contextlib import ExitStack

import concourse.bass as bass
from concourse import mybir

ALU = mybir.AluOpType
ACT = mybir.ActivationFunctionType
AX_X = mybir.AxisListType.X
F32 = mybir.dt.float32
I32 = mybir.dt.int32

IMAGES, C, SIDE = 2, 512, 64
PIXELS = SIDE * SIDE
P = 128
CT = C // P
ROWS = 8
PX = ROWS * SIDE
CHUNKS = SIDE // ROWS
PAD = SIDE + 2
MAP = PAD * PAD
GROUPS, POINTS, GC = 16, 9, 32
GP = GROUPS * POINTS
OM = 3 * GP
TILES = PX // P
KG = TILES * GROUPS
REACH = 2.0
NEAR = 5
WIN = 8
CELL = WIN * WIN * GROUPS
MARGIN = WIN // 2
BEFORE = 3
PROWS = SIDE + 7
MID = C // 2
BRANCHES, MT = 4, MID // P
TAPS = 9
NO_ROW = 4096
GN_EPS = LN_EPS = BN_EPS = 1e-5

K_MEAN, K_GROUP, K_EYE, K_BELOW, K_ONE = 0, P, 2 * P, 3 * P, 4 * P
K_IOTA = 5 * P
K_BAND = K_IOTA + 2 * C
K_INDEX = K_BAND + SIDE
K_CX = K_INDEX + 8
K_CY = K_CX + POINTS
K_SHIFT = K_CY + POINTS
K_POWER = K_SHIFT + NEAR
K_COLS = K_POWER + 1

U_MAIN, U_33 = 0, TAPS * CT
U_ONE = U_33 + TAPS * MT
U_AVG = U_ONE + CT
UNITS = U_AVG + CT
GROUPS_W = UNITS // 2
MAIN, ONE, CONV3, AVG = range(BRANCHES)
V_RANK, V_SCALE, V_BIAS, V_TSCALE, V_TBIAS, NV = 0, 1, 2, 3, 4, 5


POW_IMAGE = CHUNKS + 2


class Chain:

    def __init__(self, eng, sem):
        self.eng, self.sem, self.base, self.n = eng, sem, 0, 0

    def did(self, instruction):
        instruction.then_inc(self.sem, 1)
        self.n += 1

    def wait(self, back=0):
        self.eng.wait_ge(self.sem, self.base + self.n - back)

    def enter(self, i, per):
        self.start, self.per = self.base + self.n, per
        self.base, self.n = self.start + i * per, 0

    def leave(self, trips):
        assert self.n == self.per, (self.n, self.per)
        self.base, self.n = self.start + trips * self.per, 0


def conv_preact_program(nc, x, chan, in_w, in_b, wom, bom, out_w, w31, wmain_o, w33_o, w1_o, wa_o,
                        bn, fuse, score, score_col, consts, out):
    with ExitStack() as ctx:
        def sb(name, shape, dt=F32):
            return ctx.enter_context(nc.sbuf_tensor(name, shape, dt))

        def sem(name):
            return ctx.enter_context(nc.semaphore(name))

        def dram(name, shape):
            return nc.dram_tensor(name, shape, F32, kind="Internal").ap()

        proj_d = dram("proj_d", [PROWS, SIDE, C])
        cell_d = dram("cell_d", [PIXELS + 2 * MARGIN, CELL])
        om_d = dram("om_d", [CHUNKS, P, TILES * OM])
        samp_d = dram("samp_d", [C, PIXELS])
        mid_d = [dram(f"mid_d{n}", [C * CHUNKS, PX]) for n in range(IMAGES)]
        w_d = dram("w_d", [P, UNITS * MID])

        H = sb("H", [P, CT * MAP])
        H4 = H[:, :].rearrange("p (t y x) -> p t y x", t=CT, y=PAD)
        K = sb("K", [P, K_COLS])
        chan_sb = sb("chan_sb", [P, CT, 13])
        prm = sb("prm", [P, BRANCHES, MT, NV])
        rowidx = sb("rowidx", [P, BRANCHES * MT, IMAGES, CHUNKS], I32)
        jobidx = sb("jobidx", [P, 4, IMAGES], I32)
        t31p = sb("t31p", [P, MT, 2])
        stats = sb("stats", [P, CT, CHUNKS, 6])
        mv = sb("mv", [P, CT, 2])
        ag = sb("ag", [P, CT, 2])
        gs = sb("gs", [P, CT, 2])
        gtmp = sb("gtmp", [P, CT])
        nscale = sb("nscale", [P, CT])
        nbias = sb("nbias", [P, CT])
        amax = sb("amax", [P, CHUNKS])
        far = sb("far", [P, 2])
        farflag = sb("farflag", [P, 1], I32)
        small = sb("small", [P, 2, TILES * GROUPS])
        var = sb("var", [P, TILES])
        REGION = 32400
        R = sb("R", [P, REGION])

        def views(*shapes):
            at, made = 0, []
            for s in shapes:
                n = 1
                for d in s:
                    n *= d
                v = R[:, at:at + n]
                if len(s) > 1:
                    names = "abcdef"[:len(s)]
                    v = v.rearrange(f"p ({' '.join(names)}) -> p {' '.join(names)}",
                                    **{names[i]: s[i] for i in range(len(s))})
                made.append(v)
                at += n
            assert at <= REGION, at
            return made


        mean_w, group_w, eye, below_w, one_w = (K[:, k:k + P] for k in (K_MEAN, K_GROUP, K_EYE, K_BELOW, K_ONE))
        iota = K[:, K_IOTA:K_IOTA + 2 * C]
        band = K[:, K_BAND:K_BAND + SIDE]
        jbias = K[:, K_SHIFT:K_SHIFT + NEAR]

        ps = ctx.enter_context(nc.psum_tensor("ps", [P, 8, 512], F32))

        phase_done = sem("phase_done")
        const_in, score_in, bn_in, small_w_in, main_w_in = (sem(s) for s in ("const_in", "score_in", "bn_in", "small_w_in", "main_w_in"))
        zero_ready, zero_out, border_ready = sem("zero_ready"), sem("zero_out"), sem("border_ready")
        x_in = [sem(f"x_in{t}") for t in range(CT)]
        dve_step, act_step, pool_step = sem("dve_step"), sem("act_step"), sem("pool_step")
        sel_ready, place_ready, onehot_ready, sig_ready = sem("sel_ready"), sem("place_ready"), sem("onehot_ready"), sem("sig_ready")
        pm_ready, prm_ps = sem("pm_ready"), sem("prm_ps")
        wp_ps, wp_sb = sem("wp_ps"), sem("wp_sb")
        wp_out = [sem(f"wp_out{k}") for k in range(4)]
        ag_ready, gstat_ps, nrm_ready, h_act, h_dve = sem("ag_ready"), sem("gstat_ps"), sem("nrm_ready"), sem("h_act"), sem("h_dve")
        passed = sem("passed")
        pow_asked, pow_done = sem("pow_asked"), sem("pow_done")
        l0w_in, hc_ready = sem("l0w_in"), sem("hc_ready")
        dw_done, y2_done, stat_ps, musq_done, ln_done, gelu_done = (sem(s) for s in ("dw_done", "y2_done", "stat_ps", "musq_done", "ln_done", "gelu_done"))
        om_ps, om_ready, tent_done, exp_done, cell_ready = (sem(s) for s in ("om_ps", "om_ready", "tent_done", "exp_done", "cell_ready"))
        cell_zero, diag_ready, rstd_ps = sem("cell_zero"), sem("diag_ready"), sem("rstd_ps")
        cell_out, row_ready = sem("cell_out"), sem("row_ready")
        om_out = sem("om_out")
        xp_ps, xp_sb, xp_out = sem("xp_ps"), sem("xp_sb"), sem("xp_out")
        p_in = [sem(f"p_in{k}") for k in range(8)]
        cw_in = [sem(f"cw_in{k}") for k in range(4)]
        w_ready, w_free, s_free = sem("w_ready"), sem("w_free"), sem("s_free")
        s_out = [sem("s_out0"), sem("s_out1")]
        outw_in, flag_ps, flag_ready, far_ready = sem("outw_in"), sem("flag_ps"), sem("flag_ready"), sem("far_ready")
        so_in = [sem("so_in0"), sem("so_in1")]
        o_ps, x1_ready, x1_copied, x1_counted = sem("o_ps"), sem("x1_ready"), sem("x1_copied"), sem("x1_counted")
        x1_out = [sem("x1_out0"), sem("x1_out1")]
        l1w_in, tzero = sem("l1w_in"), sem("tzero")
        g_ps, g_free, pooled, pool_sb, job_added = (sem(s) for s in ("g_ps", "g_free", "pooled", "pool_sb", "job_added"))
        res_in = [sem(f"res_in{k}") for k in range(4)]
        res_out = [sem(f"res_out{k}") for k in range(4)]
        far_load = [sem(f"far_load{n}") for n in range(IMAGES)]
        far_step = [sem(f"far_step{n}") for n in range(IMAGES)]
        far_w = [sem(f"far_w{n}") for n in range(IMAGES)]
        far_tr = [sem(f"far_tr{n}") for n in range(IMAGES)]
        far_cp = [sem(f"far_cp{n}") for n in range(IMAGES)]
        far_mm = [sem(f"far_mm{n}") for n in range(IMAGES)]
        far_sb = [sem(f"far_sb{n}") for n in range(IMAGES)]
        far_dve = [sem(f"far_dve{n}") for n in range(IMAGES)]
        far_out = [sem(f"far_out{n}") for n in range(IMAGES)]

        (wmain_sb, w33_sb, w1_sb, wa_sb, onehot, sc_row, cmp_a, cmp_b, zeros, wstage) = views(
            [2, TAPS * C], [2, TAPS * MID], [2, C], [2, C], [BRANCHES, MT, MID], [2 * C], [2 * C], [2 * C],
            [2 * C], [4, 512])
        (in_w_sb, hc, wom_sb, bom_sb, in_b_sb, y, ge, xp, om, tents, cell, prod, diag) = views(
            [CT, C], [CT, PX], [CT, OM], [OM], [C], [CT, PX], [CT, PX], [TILES, C], [3, POINTS, KG],
            [2, POINTS, NEAR, KG], [2, TILES * CELL], [2, NEAR, NEAR, KG], [PX])
        cell_acc = cell[:, 0, :].rearrange("p (e d f) -> p e d f", e=WIN, d=WIN)
        cell_row = cell[:, 1, :].rearrange("p (k f) -> p k f", k=TILES)
        (p_ring, cw_ring, w_ring, s_buf) = views([8, C], [4, CELL], [2, SIDE, 4, GROUPS], [2, CT, PX])
        (out_w_sb, so_buf, x1_buf) = views([CT, C], [2, CT, PX], [2, CT, PX])
        (f_om, f_tx, f_ty, f_wt, f_tmp, f_x, f_col, f_out, f_pos) = views(
            [3, POINTS, KG], [POINTS, SIDE], [POINTS, SIDE], [SIDE, SIDE], [SIDE, SIDE], [SIDE // 2, GC], [512], [P], [2 * POINTS])
        (T, lw, w31_sb, rbuf, tbuf, vsum, hsum) = views(
            [MT, PAD, PAD], [UNITS, MID], [CT, MID], [4, PX], [4, PX], [ROWS, PAD], [2, PX])

        prep = sb("prep", [P, 400])
        s_col = prep[:, 0:8]
        rank = prep[:, 8:16]
        chosen = prep[:, 16:24]
        place = prep[:, 24:32]
        sig = prep[:, 32:40]
        bnp = prep[:, 40:72].rearrange("p (b k o) -> p b k o", b=4, k=4)
        bnsc = prep[:, 72:80].rearrange("p (b o) -> p b o", b=4)
        bnbi = prep[:, 80:88].rearrange("p (b o) -> p b o", b=4)
        fw = prep[:, 88:92]
        pm = prep[:, 92:132].rearrange("p (b o v) -> p b o v", b=BRANCHES, o=MT)
        base8 = prep[:, 132:140]

        def led(count):
            return count + 1

        def held(eng, semaphore, value):
            eng.wait_ge(semaphore, value)
            eng.sem_inc(passed, 1)

        def barrier(eng, k):
            eng.drain().then_inc(phase_done, 1)
            eng.wait_ge(phase_done, 5 * k)

        PH_CELLS, PH_SAMPLE, PH_FAR, PH_OUT, PH_L1 = range(5)

        def ph(n, k):
            return 2 + 5 * n + k

        block = ctx.enter_context(nc.Block())

        @block.sync
        def _(sp):
            for semaphore in (*x1_out, xp_out, cell_out, *far_out, om_out):
                sp.sem_inc(semaphore, 1)
            sp.dma_start(K[:, :], consts).then_inc(const_in, 16)
            sp.dma_start(chan_sb[:, :, :], chan).then_inc(const_in, 16)
            sp.dma_start(sc_row, score.partition_broadcast(P)).then_inc(score_in, 16)
            sp.dma_start(s_col, score_col).then_inc(score_in, 16)
            sp.dma_start(bnp, bn).then_inc(bn_in, 16)
            sp.dma_start(fw, fuse.partition_broadcast(P)).then_inc(bn_in, 16)

            def load_x(n):
                for t in range(CT):
                    sp.dma_start(H4[:, t, 1:SIDE + 1, 1:SIDE + 1],
                                 x[n, t * P:(t + 1) * P, :].rearrange("p (y x) -> p y x", y=SIDE)).then_inc(x_in[t], 16)

            load_x(0)
            sp.dma_start(w1_sb, w1_o.rearrange("(o p) c -> p o c", p=P)).then_inc(small_w_in, 16)
            sp.dma_start(wa_sb, wa_o.rearrange("(o p) c -> p o c", p=P)).then_inc(small_w_in, 16)
            sp.dma_start(w33_sb, w33_o.rearrange("(o p) c -> p o c", p=P)).then_inc(small_w_in, 16)
            sp.dma_start(wmain_sb, wmain_o.rearrange("(o p) c -> p o c", p=P)).then_inc(main_w_in, 16)
            sp.wait_ge(zero_ready, 1)
            for r in (*range(BEFORE), *range(SIDE + BEFORE, PROWS)):
                sp.dma_start(proj_d[r], zeros[0:SIDE, 0:C]).then_inc(zero_out, 16)
            for r in (0, PIXELS):
                sp.dma_start(cell_d[r:r + 2 * MARGIN, :], zeros[0:2 * MARGIN, 0:CELL]).then_inc(zero_out, 16)
            for g in range(GROUPS_W):
                sp.wait_ge(wp_sb, g + 1)
                sp.dma_start(w_d[:, g * 512:(g + 1) * 512], wstage[:, g % 4, :]).then_inc(wp_out[g % 4], 16)
            for k in range(4):
                sp.wait_ge(wp_out[k], 16 * len(range(k, GROUPS_W, 4)))
            sp.wait_ge(zero_out, 16 * (PROWS - SIDE + 2))
            barrier(sp, 1)

            for n in range(IMAGES):
                if n:
                    load_x(n)
                sp.dma_start(in_w_sb, in_w.rearrange("(t p) o -> p t o", p=P)).then_inc(l0w_in, 16)
                sp.dma_start(wom_sb, wom.rearrange("(t p) o -> p t o", p=P)).then_inc(l0w_in, 16)
                sp.dma_start(bom_sb, bom.partition_broadcast(P)).then_inc(l0w_in, 16)
                sp.dma_start(in_b_sb[0:1, :], in_b.rearrange("(a c) -> a c", a=1)).then_inc(l0w_in, 16)

                with sp.Fori(0, CHUNKS) as c:
                    cg = c + n * CHUNKS
                    sp.wait_ge(xp_sb, cg * TILES + (TILES + 2))
                    sp.dma_start(proj_d[bass.ds(c * ROWS + BEFORE, ROWS)].rearrange(
                        "(k r) x c -> (r x) k c", r=2), xp).then_inc(xp_out, 16)
                    sp.wait_ge(cell_ready, led(cg + 1))
                    sp.dma_start(om_d[bass.ds(c, 1)].rearrange("a p f -> p (a f)"), om.rearrange("p a q f -> p (a q f)")).then_inc(om_out, 16)
                    sp.wait_ge(row_ready, led(cg + 1))
                    for k in range(TILES):
                        for q in range(WIN):
                            dst = bass.AP(tensor=cell_d.tensor, offset=c * (PX * CELL) + ((k * P + q + 1) * CELL + q * P),
                                          ap=[[WIN * CELL, P // WIN], [CELL, WIN], [1, P]])
                            src = cell_row[q:P - WIN + q + 1:WIN, k, :].rearrange("p (e f) -> p e f", e=WIN)
                            sp.dma_start(dst, src).then_inc(cell_out, 16)
                sp.wait_ge(cell_out, led(16 * WIN * TILES * (n + 1) * CHUNKS))
                sp.wait_ge(xp_out, led(16 * (n + 1) * CHUNKS))
                sp.wait_ge(om_out, led(16 * (n + 1) * CHUNKS))
                barrier(sp, ph(n, PH_CELLS))

                def load_pair(m, slot):
                    sp.dma_start(p_ring[:, slot, :], proj_d[bass.ds(m, 2)].rearrange("y x c -> (y x) c")).then_inc(p_in[slot], 16)

                for m in range(6):
                    load_pair(m, m)
                with sp.Fori(0, CHUNKS) as i:
                    for s in range(ROWS):
                        yy = i * ROWS + s
                        sp.wait_ge(w_ready, yy + (n * SIDE + 1))
                        for h in range(2):
                            src = bass.AP(tensor=cell_d.tensor, offset=yy * (SIDE * CELL) + (MARGIN * CELL + h * (P // 2)),
                                          ap=[[CELL, SIDE], [1, CELL - P // 2]])
                            sp.dma_start(cw_ring[h * SIDE:(h + 1) * SIDE, s % 4, 0:CELL - P // 2], src).then_inc(cw_in[s % 4], 16)
                        sp.wait_ge(w_free, yy + (n * SIDE + 1))
                        load_pair(yy + 6, (s + 6) % 8)
                barrier(sp, ph(n, PH_SAMPLE))

                sp.wait_ge(flag_ready, n + 1)
                flag = sp.value_load(farflag[0:1, 0:1], min_val=0, max_val=1)
                with sp.If(flag > 0):
                    with sp.Fori(0, CHUNKS) as c:
                        sp.wait_ge(far_sb[n], led(c * KG))
                        sp.dma_start(f_om.rearrange("p a q f -> p (a q f)"), om_d[bass.ds(c, 1)].rearrange("a p f -> p (a f)")).then_inc(far_load[n], 16)
                        with sp.Fori(0, TILES) as k:
                            with sp.Fori(0, GROUPS) as g:
                                it = c * KG + k * GROUPS + g
                                sp.wait_ge(far_sb[n], led(it))
                                src = bass.AP(tensor=proj_d.tensor, offset=g * GC + BEFORE * SIDE * C,
                                              ap=[[C, P], [2 * SIDE * C, SIDE // 2], [1, GC]])
                                sp.dma_start(f_x, src).then_inc(far_w[n], 16)
                                sp.wait_ge(far_sb[n], led(it + 1))
                                sp.dma_start(samp_d[bass.ds(g * GC, GC), bass.ds(c * PX + k * P, P)], f_out[0:GC, :]).then_inc(far_out[n], 16)
                                held(sp, far_out[n], led(it * 16 + 16))
                    sp.wait_ge(far_out[n], led(16 * CHUNKS * TILES * GROUPS))
                barrier(sp, ph(n, PH_FAR))

                sp.dma_start(out_w_sb, out_w.rearrange("(t p) o -> p t o", p=P)).then_inc(outw_in, 16)
                with sp.Fori(0, CHUNKS // 2) as i:
                    for par in range(2):
                        c = i * 2 + par
                        cg = n * CHUNKS + c
                        sp.wait_ge(o_ps, cg + 1)
                        sp.dma_start(so_buf[:, par], samp_d[:, bass.ds(c * PX, PX)].rearrange("(t p) f -> p t f", p=P)).then_inc(so_in[par], 16)
                        held(sp, x1_copied, cg + 1)
                        held(sp, x1_counted, cg + 1)
                        sp.wait_ge(x1_out[par], led((n * (CHUNKS // 2) + i) * 16))
                        sp.dma_start(x1_buf[:, par], x[n, :, bass.ds(c * PX, PX)].rearrange("(t p) f -> p t f", p=P)).then_inc(so_in[par], 16)
                        sp.wait_ge(x1_ready, cg + 3)
                        dst = bass.AP(tensor=mid_d[n].tensor, offset=c * PX,
                                      ap=[[PIXELS, P], [P * PIXELS, CT], [1, PX]])
                        sp.dma_start(dst, x1_buf[:, par]).then_inc(x1_out[par], 16)
                for par in range(2):
                    sp.wait_ge(x1_out[par], led(16 * (n + 1) * CHUNKS // 2))
                barrier(sp, ph(n, PH_OUT))

                sp.dma_start(lw, w_d.rearrange("p (u f) -> p u f", u=UNITS)).then_inc(l1w_in, 16)
                sp.dma_start(w31_sb, w31.rearrange("(t p) o -> p t o", p=P)).then_inc(l1w_in, 16)
                barrier(sp, ph(n, PH_L1))

        @block.gpsimd
        def _(pool):
            chain = Chain(pool, pool_step)
            pool.memset(zeros, 0.0).then_inc(zero_ready, 1)
            for edge in (H4[:, :, 0, :], H4[:, :, PAD - 1, :], H4[:, :, 1:PAD - 1, 0], H4[:, :, 1:PAD - 1, PAD - 1]):
                pool.memset(edge, 0.0).then_inc(border_ready, 1)

            def inverse_root(v, width, k):
                pool.wait_ge(pow_asked, k)
                pool.tensor_tensor(v, v, K[:, K_POWER:K_POWER + 1].to_broadcast([P, width]), ALU.pow).then_inc(pow_done, 1)

            inverse_root(prep[:, 72:80], 8, 1)
            inverse_root(nscale[:, :], CT, 2)
            barrier(pool, 1)
            for n in range(IMAGES):
                if n:
                    inverse_root(nscale[:, :], CT, POW_IMAGE * n + 2)
                with pool.Fori(0, CHUNKS) as c:
                    inverse_root(var[:, :], TILES, c + (POW_IMAGE * n + 3))
                    held(pool, row_ready, led(c + n * CHUNKS))
                    pool.memset(cell_acc, 0.0).then_inc(cell_zero, 1)
                barrier(pool, ph(n, PH_CELLS))
                barrier(pool, ph(n, PH_SAMPLE))
                barrier(pool, ph(n, PH_FAR))
                inverse_root(nscale[:, :], CT, POW_IMAGE * n + 3 + CHUNKS)
                barrier(pool, ph(n, PH_OUT))

                for edge in (T[:, :, 0, :], T[:, :, PAD - 1, :], T[:, :, 1:PAD - 1, 0], T[:, :, 1:PAD - 1, PAD - 1]):
                    pool.memset(edge, 0.0).then_inc(tzero, 1)
                pool.memset(rbuf, 0.0).then_inc(tzero, 1)
                pool.wait_ge(tzero, 5 * (n + 1))

                def gather(bm, cc, slot):
                    chain.did(pool.tensor_copy(jobidx[:, slot, :], rowidx[:, bm, :, bass.ds(cc, 1)].rearrange("p n a -> p (n a)")))
                    held(pool, pool_step, chain.base + chain.n)
                    pool.indirect_dma_start(
                        out=rbuf[:, slot, :], out_offset=None, in_=mid_d[n],
                        in_offset=bass.IndirectOffsetOnAxis(ap=jobidx[:, slot, 0:1], axis=0),
                        bounds_check=C * CHUNKS - 1, oob_is_err=False).then_inc(res_in[slot], 16)

                def scatter(slot, job):
                    held(pool, job_added, job + 5)
                    pool.indirect_dma_start(
                        out=out, out_offset=bass.IndirectOffsetOnAxis(ap=jobidx[:, slot, n:n + 1], axis=0),
                        in_=rbuf[:, slot, :], in_offset=None,
                        bounds_check=IMAGES * C * CHUNKS - 1, oob_is_err=False).then_inc(res_out[slot], 16)

                base = n * 64
                lists = []
                lists.append(([(ONE, 0), (ONE, 1), (AVG, 0), (AVG, 1)], 8, lambda i: [i, i, i, i]))
                lists.append(([(MAIN, 0), (MAIN, 1), (MAIN, 0), (MAIN, 1)], 4, lambda i: [i * 2, i * 2, i * 2 + 1, i * 2 + 1]))
                lists.append(([(CONV3, 0), (CONV3, 1), (CONV3, 0), (CONV3, 1)], 4, lambda i: [i * 2, i * 2, i * 2 + 1, i * 2 + 1]))
                for kinds, trips, ccs in lists:
                    def four_jobs(i, first):
                        quad = i + base // 4
                        for k in range(4):
                            b, m = kinds[k]
                            if not first:
                                held(pool, res_out[k], quad * 16)
                            gather(b * MT + m, ccs(i)[k], k)
                            if k >= 2:
                                scatter(k - 2, quad * 4 + k - 2)
                        scatter(2, quad * 4 + 2)
                        scatter(3, quad * 4 + 3)

                    peeled = 1 if base == 0 else 0
                    if peeled:
                        four_jobs(0, True)
                    with pool.Fori(peeled, trips) as i:
                        chain.enter(i - peeled, 4)
                        four_jobs(i, False)
                    chain.leave(trips - peeled)
                    base += 4 * trips
                for k in range(4):
                    pool.wait_ge(res_out[k], 16 * 16 * (n + 1))
                barrier(pool, ph(n, PH_L1))

        @block.scalar
        def _(act):
            chain = Chain(act, act_step)
            act.drain().then_inc(xp_sb, 2)
            for semaphore in (row_ready, pool_sb, *s_out):
                act.sem_inc(semaphore, 1)
            act.drain().then_inc(s_free, 4)
            act.drain().then_inc(g_free, 4)
            act.drain().then_inc(x1_copied, 2)
            act.wait_ge(const_in, 32)
            act.wait_ge(score_in, 32)
            act.activation(sig, s_col, ACT.Sigmoid).then_inc(sig_ready, 1)
            for g in range(GROUPS_W):
                act.wait_ge(wp_ps, g + 1)
                if g >= 4:
                    act.wait_ge(wp_out[g % 4], 16 * (g // 4))
                act.activation(wstage[:, g % 4, :], ps[:, g % 4, :], ACT.Copy).then_inc(wp_sb, 1)

            def normalise(k):
                act.wait_ge(nrm_ready, k)
                for t in range(2):
                    v = H4[:, t, 1:SIDE + 1, 1:SIDE + 1]
                    act.activation(v, v, ACT.Identity, bias=nbias[:, t:t + 1], scale=nscale[:, t:t + 1]).then_inc(h_act, 1)

            normalise(1)
            barrier(act, 1)
            for n in range(IMAGES):
                if n:
                    normalise(2 * n + 1)

                def head(c, cg):
                    act.wait_ge(dw_done, cg + 1)
                    act.wait_ge(om_ps, led(TILES * cg))
                    act.activation(ge, y, ACT.Square).then_inc(y2_done, 1)
                    act.wait_ge(xp_ps, led(TILES * cg))
                    for t in range(CT):
                        ins = act.activation(hc[:, t, :].rearrange("p (y x) -> p y x", y=ROWS),
                                             H4[:, t, bass.ds(c * ROWS + 1, ROWS), 1:SIDE + 1], ACT.Copy)
                    ins.then_inc(hc_ready, 1)
                    act.wait_ge(stat_ps, cg + 1)
                    act.activation(diag, ps[:, 2, 0:PX], ACT.Square).then_inc(musq_done, 1)
                    for k in range(TILES):
                        act.wait_ge(xp_ps, led(TILES * cg + k + 1))
                        if k == 0:
                            act.wait_ge(xp_out, led(cg * 16))
                        act.activation(xp[:, k, :], ps[:, k % 2, :], ACT.Copy).then_inc(xp_sb, 1)
                    act.wait_ge(ln_done, led(cg + 1))
                    for t in range(CT):
                        act.activation(ge[:, t, :], ge[:, t, :], ACT.Gelu, bias=chan_sb[:, t, 11:12], scale=chan_sb[:, t, 10:11]).then_inc(gelu_done, 1)

                def cells(c, cg, last):
                    act.wait_ge(om_ready, led(cg + 1))
                    act.wait_ge(cell_ready, led(cg))
                    for j in range(NEAR):
                        ins = act.activation(
                            tents.rearrange("p a q j f -> p (a q) j f")[:, :, j, :],
                            om[:, 0:2].rearrange("p a q f -> p (a q) f"),
                            ACT.Abs, bias=jbias[:, j:j + 1])
                        chain.did(ins)
                    chain.wait()
                    act.activation(tents, tents, ACT.Relu, bias=jbias[:, 1:2], scale=-1.0).then_inc(tent_done, 1)
                    act.activation(om[:, 2], om[:, 2], ACT.Exp).then_inc(exp_done, 1)
                    if not last:
                        head(c + 1, cg + 1)
                    act.wait_ge(cell_ready, led(cg + 1))
                    act.wait_ge(cell_out, led(cg * (16 * WIN * TILES)))
                    for k in range(TILES):
                        for h in range(2):
                            dst = cell_row[:, k].rearrange("p (e h t g) -> p e h t g", e=WIN, h=2, g=GROUPS)[:, :, h]
                            src = cell_acc.rearrange("p e (t h) (k g) -> p e t h k g", h=2, g=GROUPS)[:, :, :, h, k]
                            ins = act.activation(dst, src, ACT.Copy)
                    ins.then_inc(row_ready, 1)

                head(0, n * CHUNKS)
                with act.Fori(0, CHUNKS - 1) as c:
                    chain.enter(c, NEAR)
                    cells(c, c + n * CHUNKS, False)
                chain.leave(CHUNKS - 1)
                cells(CHUNKS - 1, n * CHUNKS + CHUNKS - 1, True)
                barrier(act, ph(n, PH_CELLS))

                with act.Fori(0, CHUNKS // 2) as i:
                    for par in range(2):
                        cg = i * 2 + (n * CHUNKS + par)
                        act.wait_ge(s_out[par], led((n * (CHUNKS // 2) + i) * 16))
                        for pr in range(4):
                            act.wait_ge(w_free, cg * ROWS + 2 * pr + 4)
                            act.activation(s_buf[:, par, :, pr * P:(pr + 1) * P],
                                           ps[:, pr, :].rearrange("p (t f) -> p t f", t=CT), ACT.Copy).then_inc(s_free, 1)
                        act.wait_ge(s_free, cg * 4 + 4 + 4)
                        act.dma_start(samp_d[:, bass.ds((i * 2 + par) * PX, PX)].rearrange("(t p) f -> p t f", p=P),
                                      s_buf[:, par]).then_inc(s_out[par], 16)
                for par in range(2):
                    act.wait_ge(s_out[par], led(16 * (n + 1) * CHUNKS // 2))
                barrier(act, ph(n, PH_SAMPLE))
                barrier(act, ph(n, PH_FAR))

                with act.Fori(0, CHUNKS // 2) as i:
                    for par in range(2):
                        c = i * 2 + par
                        act.wait_ge(x1_ready, c + n * CHUNKS + 3)
                        for t in range(CT):
                            ins = act.activation(H4[:, t, bass.ds(c * ROWS + 1, ROWS), 1:SIDE + 1],
                                           x1_buf[:, par, t, :].rearrange("p (y x) -> p y x", y=ROWS), ACT.Copy)
                        ins.then_inc(x1_copied, 1)
                normalise(2 * n + 2)
                barrier(act, ph(n, PH_OUT))

                act.wait_ge(tzero, 5 * (n + 1))
                gbase = n * 80

                def to_map(prow, g0):
                    with act.Fori(0, CHUNKS // 2) as i:
                        for s in range(2):
                            for m in range(MT):
                                act.wait_ge(g_ps, i * 4 + (g0 + 2 * s + m + 1))
                                sc, bi = prow(m)
                                act.activation(T[:, m, bass.ds((i * 2 + s) * ROWS + 1, ROWS), 1:SIDE + 1],
                                               ps[:, 2 * s + m, :].rearrange("p (y x) -> p y x", y=ROWS),
                                               ACT.Identity, bias=bi, scale=sc).then_inc(g_free, 1)

                to_map(lambda m: (prm[:, AVG, m, V_TSCALE:V_TSCALE + 1], prm[:, AVG, m, V_TBIAS:V_TBIAS + 1]), gbase)
                jbase = n * 64

                def finish(b, m, bank, group, job, slot):
                    act.wait_ge(g_ps, group + 1)
                    act.wait_ge(job_added, job + 1)
                    act.activation(tbuf[:, slot, :], ps[:, bank, :], ACT.Identity, bias=prm[:, b, m, V_BIAS:V_BIAS + 1],
                                   scale=prm[:, b, m, V_SCALE:V_SCALE + 1]).then_inc(g_free, 1)

                with act.Fori(0, CHUNKS // 2) as i:
                    for s in range(2):
                        for m in range(MT):
                            finish(ONE, m, 2 * s + m, i * 4 + (gbase + 16 + 2 * s + m), i * 8 + (jbase + 4 * s + m), m)
                        for m in range(MT):
                            act.wait_ge(pooled, i * 4 + (n * 16 + 2 * s + m + 1))
                            act.wait_ge(job_added, i * 8 + (jbase + 4 * s + 2 + m + 1))
                            act.activation(tbuf[:, 2 + m, :], hsum[:, m, :], ACT.Identity, bias=prm[:, AVG, m, V_BIAS:V_BIAS + 1],
                                           scale=prm[:, AVG, m, V_SCALE:V_SCALE + 1]).then_inc(pool_sb, 1)
                with act.Fori(0, CHUNKS // 2) as i:
                    for k in range(4):
                        finish(MAIN, k % 2, k, i * 4 + (gbase + 32 + k), i * 4 + (jbase + 32 + k), k)
                act.wait_ge(pooled, 2 * CHUNKS * (n + 1))
                to_map(lambda m: (t31p[:, m, 0:1], t31p[:, m, 1:2]), gbase + 48)
                with act.Fori(0, CHUNKS // 2) as i:
                    for k in range(4):
                        finish(CONV3, k % 2, k, i * 4 + (gbase + 64 + k), i * 4 + (jbase + 48 + k), k)
                barrier(act, ph(n, PH_L1))

        @block.tensor
        def _(pe):
            pe.drain().then_inc(w_free, 2)
            for semaphore in (om_ps, xp_ps, *far_mm):
                pe.sem_inc(semaphore, 1)
            pe.drain().then_inc(o_ps, 2)
            pe.wait_ge(const_in, 32)
            pe.wait_ge(sel_ready, 1)
            pc = ps[:, 6, 0:8].rearrange("p (b o) -> p b o", b=BRANCHES)
            ch = chosen.rearrange("p (b o) -> p b o", b=BRANCHES)
            pe.matmul(pc[:, :, 0], below_w, ch[:, :, 0], start=True, stop=True)
            pe.matmul(pc[:, :, 1], below_w, ch[:, :, 1], start=True, stop=False)
            pe.matmul(pc[:, :, 1], one_w, ch[:, :, 0], start=False, stop=True).then_inc(place_ready, 1)
            pe.wait_ge(onehot_ready, 8)
            units = []
            for tap in range(TAPS):
                for t in range(CT):
                    units.append((MAIN, wmain_sb, tap * C + t * P))
            for tap in range(TAPS):
                for t in range(MT):
                    units.append((CONV3, w33_sb, tap * MID + t * P))
            units += [(ONE, w1_sb, t * P) for t in range(CT)]
            units += [(AVG, wa_sb, t * P) for t in range(CT)]
            pe.wait_ge(main_w_in, 16)
            pe.wait_ge(small_w_in, 48)
            for g in range(GROUPS_W):
                if g >= 4:
                    pe.wait_ge(wp_sb, g - 3)
                for h in range(2):
                    b, w, at = units[2 * g + h]
                    for o in range(MT):
                        ins = pe.matmul(ps[:, g % 4, h * MID:(h + 1) * MID], w[:, o, at:at + P], onehot[:, b, o, :],
                                        start=(o == 0), stop=(o == MT - 1))
                ins.then_inc(wp_ps, 1)
            pe.wait_ge(pm_ready, 1)
            pp = ps[:, 5, 0:BRANCHES * MT * NV].rearrange("p (b m v) -> p b m v", b=BRANCHES, m=MT)
            for b in range(BRANCHES):
                for m in range(MT):
                    for o in range(MT):
                        ins = pe.matmul(pp[:, b, m, :], onehot[:, b, o, m * P:(m + 1) * P], pm[:, b, o, :],
                                        start=(o == 0), stop=(o == MT - 1))
            ins.then_inc(prm_ps, 1)

            def group_mean(k):
                pe.wait_ge(ag_ready, k)
                pe.matmul(ps[:, 7, 0:2 * CT], group_w, ag[:, :, :].rearrange("p t v -> p (t v)"), start=True, stop=True).then_inc(gstat_ps, 1)

            group_mean(1)
            barrier(pe, 1)
            for n in range(IMAGES):
                if n:
                    group_mean(2 * n + 1)
                pe.wait_ge(h_act, 2 * (2 * n + 1))
                pe.wait_ge(h_dve, 2 * (2 * n + 1))
                pe.wait_ge(l0w_in, 64 * (n + 1))

                with pe.Fori(0, CHUNKS) as c:
                    cg = c + n * CHUNKS
                    pe.wait_ge(y2_done, cg + 1)
                    pe.wait_ge(ln_done, led(cg))
                    for bank, src in ((2, y), (3, ge)):
                        for t in range(CT):
                            ins = pe.matmul(ps[:, bank, 0:PX], mean_w, src[:, t, :], start=(t == 0), stop=(t == CT - 1))
                    ins.then_inc(stat_ps, 1)
                    pe.wait_ge(hc_ready, cg + 1)
                    for k in range(TILES):
                        pe.wait_ge(xp_sb, cg * TILES + (k + 1))
                        bank = ps[:, k % 2, :]
                        for t in range(CT):
                            pe.matmul(bank, hc[:, t, k * P:(k + 1) * P], in_w_sb[:, t, :],
                                      start=(t == 0), stop=False)
                        pe.matmul(bank, one_w[0:1, :], in_b_sb[0:1, :], start=False, stop=True).then_inc(xp_ps, 1)
                    pe.wait_ge(diag_ready, cg + 1)
                    pe.matmul(ps[:, 6, 0:PX], one_w, diag, start=True, stop=True).then_inc(rstd_ps, 1)
                    pe.wait_ge(gelu_done, cg * CT + CT)
                    pe.wait_ge(om_ready, led(cg))
                    for k in range(TILES):
                        for t in range(CT):
                            ins = pe.matmul(ps[:, 4 + k, 0:OM], ge[:, t, k * P:(k + 1) * P], wom_sb[:, t, :],
                                            start=(t == 0), stop=(t == CT - 1))
                        ins.then_inc(om_ps, 1)
                barrier(pe, ph(n, PH_CELLS))

                with pe.Fori(0, CHUNKS) as i:
                    for s in range(ROWS):
                        yg = i * ROWS + (n * SIDE + s)
                        pr, half = s // 2, s % 2
                        if half == 0:
                            pe.wait_ge(s_free, i * 4 + (n * 4 * CHUNKS + pr + 1))
                        pe.wait_ge(w_ready, yg + 5)
                        for t in range(4):
                            slot, uses = (s + 2 * t) % 8, (s + 2 * t) // 8 + 1
                            before = n * len(range(slot, SIDE + 6, 8))
                            pe.wait_ge(p_in[slot], i * 16 + 16 * (uses + before))
                        for ct in range(CT):
                            for t in range(4):
                                slot = (s + 2 * t) % 8
                                for j in range(4):
                                    g = ct * 4 + j
                                    ins = pe.matmul(ps[j * GC:(j + 1) * GC, pr, ct * P + half * SIDE:ct * P + (half + 1) * SIDE],
                                                    p_ring[:, slot, g * GC:(g + 1) * GC], w_ring[:, s % 2, :, t, g],
                                                    start=(t == 0), stop=(t == 3))
                        ins.then_inc(w_free, 1)
                pe.wait_ge(far_ready, n + 1)
                pe.matmul(ps[:, 6, 0:1], one_w, far[:, 0:1], start=True, stop=True).then_inc(flag_ps, 1)
                barrier(pe, ph(n, PH_SAMPLE))

                pe.wait_ge(flag_ready, n + 1)
                flag = pe.value_load(farflag[0:1, 0:1], min_val=0, max_val=1)
                with pe.If(flag > 0):
                    with pe.Fori(0, CHUNKS * TILES * GROUPS) as it:
                        pe.wait_ge(far_w[n], it * 16 + 16)
                        pe.wait_ge(far_step[n], it + 1)
                        for b in range(8):
                            bb = it * 8 + b
                            pe.wait_ge(far_cp[n], led(bb))
                            for k in range(4):
                                ins = pe.transpose(ps[:, 4, k * P:(k + 1) * P],
                                                   f_wt[:, 2 * (4 * b + k):2 * (4 * b + k) + 2, :].rearrange("p y x -> p (y x)"), eye)
                            ins.then_inc(far_tr[n], 1)
                            pe.wait_ge(far_cp[n], led(bb + 1))
                            if b == 0:
                                pe.wait_ge(far_sb[n], led(it))
                            for k in range(4):
                                ins = pe.matmul(ps[0:GC, 5, 0:P], f_x[:, 4 * b + k, :], f_col[:, k * P:(k + 1) * P],
                                                start=(b == 0 and k == 0), stop=(b == 7 and k == 3))
                            ins.then_inc(far_mm[n], 1)
                barrier(pe, ph(n, PH_FAR))

                pe.wait_ge(outw_in, 16 * (n + 1))
                with pe.Fori(0, CHUNKS // 2) as i:
                    for par in range(2):
                        cg = i * 2 + (n * CHUNKS + par)
                        pe.wait_ge(so_in[par], i * 32 + 32 * (n * CHUNKS // 2 + 1))
                        pe.wait_ge(x1_ready, cg + 1)
                        for o in range(CT):
                            for t in range(CT):
                                ins = pe.matmul(ps[:, 4 * par + o, :], out_w_sb[:, t, o * P:(o + 1) * P], so_buf[:, par, t, :],
                                                start=(t == 0), stop=(t == CT - 1))
                        ins.then_inc(o_ps, 1)
                group_mean(2 * n + 2)
                barrier(pe, ph(n, PH_OUT))

                pe.wait_ge(l1w_in, 32 * (n + 1))
                pe.wait_ge(h_act, 2 * (2 * n + 2))
                pe.wait_ge(h_dve, 2 * (2 * n + 2))
                gbase = n * 80

                def products(g0, terms):
                    with pe.Fori(0, CHUNKS // 2) as i:
                        for s in range(2):
                            for m in range(MT):
                                pe.wait_ge(g_free, i * 4 + (g0 + 2 * s + m + 1))
                                row = i * (2 * ROWS) + s * ROWS
                                ts = terms(m)
                                for q, (w, src, t, ky, kx) in enumerate(ts):
                                    ins = pe.matmul(ps[:, 2 * s + m, :], w, src[:, t, bass.ds(row + ky, ROWS), kx:kx + SIDE],
                                                    start=(q == 0), stop=(q == len(ts) - 1))
                                ins.then_inc(g_ps, 1)

                products(gbase, lambda m: [(lw[:, U_AVG + t, m * P:(m + 1) * P], H4, t, 1, 1) for t in range(CT)])
                products(gbase + 16, lambda m: [(lw[:, U_ONE + t, m * P:(m + 1) * P], H4, t, 1, 1) for t in range(CT)])
                products(gbase + 32, lambda m: [(lw[:, U_MAIN + tap * CT + t, m * P:(m + 1) * P], H4, t, tap // 3, tap % 3)
                                                for tap in range(TAPS) for t in range(CT)])
                products(gbase + 48, lambda m: [(w31_sb[:, t, m * P:(m + 1) * P], H4, t, 1, 1) for t in range(CT)])
                pe.wait_ge(g_free, gbase + 64 + 4)
                products(gbase + 64, lambda m: [(lw[:, U_33 + tap * MT + t, m * P:(m + 1) * P], T, t, tap // 3, tap % 3)
                                                for tap in range(TAPS) for t in range(MT)])
                barrier(pe, ph(n, PH_L1))

        @block.vector
        def _(dve):
            chain = Chain(dve, dve_step)

            def step(ins):
                chain.did(ins)
                chain.wait()

            dve.drain().then_inc(w_ready, 4)
            for semaphore in (cell_ready, ln_done, om_ready, *far_cp, *far_sb):
                dve.sem_inc(semaphore, 1)
            dve.drain().then_inc(x1_ready, 2)
            dve.drain().then_inc(x1_counted, 2)
            dve.drain().then_inc(job_added, 4)

            dve.wait_ge(const_in, 32)
            dve.wait_ge(score_in, 32)
            for t in range(8):
                step(dve.tensor_scalar(cmp_a, iota, K[:, K_INDEX + t:K_INDEX + t + 1], None, ALU.is_lt))
                step(dve.scalar_tensor_tensor(out=cmp_b, in0=sc_row, scalar=s_col[:, t:t + 1], in1=cmp_a, op0=ALU.is_equal, op1=ALU.mult))
                step(dve.scalar_tensor_tensor(out=cmp_a, in0=sc_row, scalar=s_col[:, t:t + 1], in1=cmp_b, op0=ALU.is_gt, op1=ALU.add))
                step(dve.tensor_reduce(rank[:, t:t + 1], cmp_a, AX_X, ALU.add))
            dve.tensor_scalar(chosen, rank, float(C), None, ALU.is_lt).then_inc(sel_ready, 1)
            dve.wait_ge(sel_ready, 1)
            dve.wait_ge(place_ready, 1)
            step(dve.tensor_copy(place, ps[:, 6, 0:8]))
            for b in range(BRANCHES):
                for o in range(MT):
                    k = b * MT + o
                    dve.tensor_scalar(onehot[:, b, o, :], iota[:, 0:MID], place[:, k:k + 1], chosen[:, k:k + 1],
                                      ALU.is_equal, ALU.mult).then_inc(onehot_ready, 1)
            dve.wait_ge(bn_in, 32)
            dve.tensor_scalar(bnsc, bnp[:, :, 3, :], BN_EPS, None, ALU.add).then_inc(pow_asked, 1)
            dve.wait_ge(pow_done, 1)
            step(dve.tensor_tensor(bnsc, bnsc, bnp[:, :, 0, :], ALU.mult))
            step(dve.tensor_tensor(bnbi, bnsc, bnp[:, :, 1 + 1, :], ALU.mult))
            step(dve.tensor_tensor(bnbi, bnp[:, :, 1, :], bnbi, ALU.subtract))
            B31, B33, BA1, BA2 = range(4)
            step(dve.tensor_scalar(t31p[:, :, 0], bnsc[:, B31], fw[:, 2:3], None, ALU.mult))
            step(dve.tensor_copy(t31p[:, :, 1], bnbi[:, B31]))
            step(dve.memset(pm, 0.0))
            rk = rank.rearrange("p (b o) -> p b o", b=BRANCHES)
            dve.wait_ge(sig_ready, 1)
            sg = sig.rearrange("p (b o) -> p b o", b=BRANCHES)
            step(dve.tensor_scalar(pm[:, :, :, V_RANK], rk, -1.0, float(NO_ROW), ALU.mult, ALU.add))
            step(dve.tensor_scalar(pm[:, MAIN, :, V_SCALE], sg[:, MAIN], fw[:, 0:1], None, ALU.mult))
            step(dve.tensor_scalar(pm[:, ONE, :, V_SCALE], sg[:, ONE], fw[:, 1:2], None, ALU.mult))
            step(dve.tensor_tensor(pm[:, CONV3, :, V_SCALE], sg[:, CONV3], bnsc[:, B33], ALU.mult))
            step(dve.tensor_tensor(pm[:, CONV3, :, V_BIAS], sg[:, CONV3], bnbi[:, B33], ALU.mult))
            step(dve.scalar_tensor_tensor(out=pm[:, AVG, :, V_SCALE], in0=sg[:, AVG], scalar=1.0 / 9.0, in1=bnsc[:, BA2], op0=ALU.mult, op1=ALU.mult))
            step(dve.tensor_tensor(pm[:, AVG, :, V_BIAS], sg[:, AVG], bnbi[:, BA2], ALU.mult))
            step(dve.tensor_scalar(pm[:, AVG, :, V_TSCALE], bnsc[:, BA1], fw[:, 3:4], None, ALU.mult))
            dve.tensor_copy(pm[:, AVG, :, V_TBIAS], bnbi[:, BA1]).then_inc(pm_ready, 1)
            dve.wait_ge(prm_ps, 1)
            step(dve.tensor_copy(prm[:, :, :, :], ps[:, 5, 0:BRANCHES * MT * NV].rearrange("p (b m v) -> p b m v", b=BRANCHES, m=MT)))
            step(dve.tensor_scalar(base8, prm[:, :, :, V_RANK].rearrange("p b m -> p (b m)"), -float(CHUNKS), float(NO_ROW * CHUNKS), ALU.mult, ALU.add))
            for n in range(IMAGES):
                for c in range(CHUNKS):
                    ins = dve.tensor_scalar(rowidx[:, :, n, c], base8, float(n * C * CHUNKS + c), None, ALU.add)
            step(ins)

            def group_norm(k, kp):
                for t in range(CT):
                    chain.did(dve.bn_aggr(mv[:, t, :], stats[:, t].rearrange("p c s -> p (c s)")))
                chain.wait()
                step(dve.tensor_copy(ag[:, :, 0], mv[:, :, 0]))
                step(dve.tensor_tensor(ag[:, :, 1], mv[:, :, 0], mv[:, :, 0], ALU.mult))
                dve.tensor_tensor(ag[:, :, 1], ag[:, :, 1], mv[:, :, 1], ALU.add).then_inc(ag_ready, 1)
                dve.wait_ge(gstat_ps, k)
                step(dve.tensor_copy(gs[:, :, :], ps[:, 7, 0:2 * CT].rearrange("p (t v) -> p t v", v=2)))
                step(dve.tensor_tensor(gtmp[:, :], gs[:, :, 0], gs[:, :, 0], ALU.mult))
                step(dve.tensor_tensor(gtmp[:, :], gs[:, :, 1], gtmp[:, :], ALU.subtract))
                dve.tensor_scalar(nscale[:, :], gtmp[:, :], GN_EPS, None, ALU.add).then_inc(pow_asked, 1)
                dve.wait_ge(pow_done, kp)
                dve.scalar_tensor_tensor(out=nbias[:, :], in0=gs[:, :, 0], scalar=-1.0, in1=nscale[:, :], op0=ALU.mult, op1=ALU.mult).then_inc(nrm_ready, 1)
                dve.wait_ge(nrm_ready, k)
                for t in range(2, CT):
                    v = H4[:, t, 1:SIDE + 1, 1:SIDE + 1]
                    dve.tensor_scalar(v, v, nscale[:, t:t + 1], nbias[:, t:t + 1], ALU.mult, ALU.add).then_inc(h_dve, 1)

            def norm_x(n):
                for t in range(CT):
                    dve.wait_ge(x_in[t], 16 * (n + 1))
                    for c in range(CHUNKS):
                        ins = dve.bn_stats(stats[:, t, c, :], H4[:, t, 1 + c * ROWS:1 + (c + 1) * ROWS, 1:SIDE + 1])
                step(ins)
                group_norm(2 * n + 1, POW_IMAGE * n + 2)

            norm_x(0)
            dve.wait_ge(border_ready, 4)
            barrier(dve, 1)

            for n in range(IMAGES):
                if n:
                    norm_x(n)
                dve.wait_ge(h_dve, 2 * (2 * n + 1))
                dve.wait_ge(h_act, 2 * (2 * n + 1))
                dve.wait_ge(l0w_in, 64 * (n + 1))

                def depthwise(c, ts):
                    for tap in range(TAPS):
                        for t in ts:
                            src = H4[:, t, bass.ds(c * ROWS + tap // 3, ROWS), tap % 3:tap % 3 + SIDE]
                            dst = y[:, t, :].rearrange("p (y x) -> p y x", y=ROWS)
                            w = chan_sb[:, t, tap:tap + 1]
                            if tap == 0:
                                ins = dve.tensor_scalar(dst, src, w, chan_sb[:, t, 9:10], ALU.mult, ALU.add)
                            else:
                                chain.wait(1)
                                ins = dve.scalar_tensor_tensor(out=dst, in0=src, scalar=w, in1=dst, op0=ALU.mult, op1=ALU.add)
                            chain.did(ins)

                diag2, eye2 = diag.rearrange("p (k f) -> p k f", k=TILES), eye.unsqueeze(1).to_broadcast([P, TILES, P])

                def variances(cg):
                    dve.wait_ge(stat_ps, cg + 1)
                    dve.wait_ge(musq_done, cg + 1)
                    step(dve.tensor_tensor(diag, ps[:, 3, 0:PX], diag, ALU.subtract))
                    step(dve.tensor_tensor(diag2, diag2, eye2, ALU.mult))
                    step(dve.tensor_reduce(var[:, :], diag2, AX_X, ALU.add))
                    dve.tensor_scalar(var[:, :], var[:, :], LN_EPS, None, ALU.add).then_inc(pow_asked, 1)

                def centre(cg):
                    dve.wait_ge(pow_done, cg + (2 * n + 3))
                    dve.tensor_tensor(diag2, var[:, :].unsqueeze(2).to_broadcast([P, TILES, P]), eye2, ALU.mult).then_inc(diag_ready, 1)
                    step(dve.tensor_tensor(ge, y, ps[:, 2, 0:PX].unsqueeze(1).to_broadcast([P, CT, PX]), ALU.subtract))

                def normalise_pixels(cg):
                    dve.wait_ge(rstd_ps, cg + 1)
                    dve.tensor_tensor(ge, ge, ps[:, 6, 0:PX].unsqueeze(1).to_broadcast([P, CT, PX]), ALU.mult).then_inc(ln_done, 1)

                def cells(c, cg, last):
                    dve.wait_ge(om_out, led(cg * 16))
                    for k in range(TILES):
                        dve.wait_ge(om_ps, led(cg * TILES + k + 1))
                        chain.did(dve.tensor_tensor(
                            om.rearrange("p a q (k g) -> p (a q) k g", k=TILES)[:, :, k, :],
                            ps[:, 4 + k, 0:OM].rearrange("p (a g) -> p a g", g=GROUPS), bom_sb.rearrange("p (a g) -> p a g", g=GROUPS), ALU.add))
                    chain.wait()
                    logits, by_group = om[:, 2], om[:, 2].rearrange("p q f -> p f q")
                    sm, sr = small[:, 0, :], small[:, 1, :]
                    smb, srb = (v.unsqueeze(1).to_broadcast([P, POINTS, KG]) for v in (sm, sr))
                    step(dve.tensor_reduce(sm, by_group, AX_X, ALU.max))
                    chain.did(dve.tensor_reduce(amax[:, bass.ds(c, 1)], om[:, 0:2].rearrange("p a q f -> p (a q f)"), AX_X, ALU.max, apply_absolute_value=True))
                    dve.tensor_tensor(logits, logits, smb, ALU.subtract).then_inc(om_ready, 1)
                    if not last:
                        depthwise(c + 1, (0, 1))
                        depthwise(c + 1, (2, 3))
                        chain.wait()
                        dve.sem_inc(dw_done, 1)
                    dve.wait_ge(exp_done, cg + 1)
                    step(dve.tensor_reduce(sm, by_group, AX_X, ALU.add))
                    step(dve.reciprocal(sr, sm))
                    step(dve.tensor_tensor(logits, logits, srb, ALU.mult))
                    dve.wait_ge(tent_done, cg + 1)
                    ty = tents[:, 1]
                    step(dve.tensor_tensor(ty, ty, logits.unsqueeze(2).to_broadcast([P, POINTS, NEAR, KG]), ALU.mult))
                    dve.wait_ge(cell_zero, cg + 1)

                    def product(q):
                        tx = tents[:, 0, q].unsqueeze(2).to_broadcast([P, NEAR, NEAR, KG])
                        u = tents[:, 1, q].unsqueeze(1).to_broadcast([P, NEAR, NEAR, KG])
                        chain.did(dve.tensor_tensor(prod[:, q % 2], tx, u, ALU.mult))

                    def sum_into(q):
                        gx, gy = q // 3, q % 3
                        acc = cell_acc[:, gx:gx + NEAR, gy:gy + NEAR, :]
                        return dve.tensor_tensor(acc, acc, prod[:, q % 2], ALU.add)

                    product(0)
                    for q in range(POINTS):
                        if not last and q == 4:
                            variances(cg + 1)
                        if not last and q == 5:
                            centre(cg + 1)
                        if not last and q == 6:
                            normalise_pixels(cg + 1)
                        if q + 1 < POINTS:
                            if q:
                                chain.wait()
                            product(q + 1)
                            chain.wait(1)
                            chain.did(sum_into(q))
                        else:
                            chain.wait()
                            sum_into(q).then_inc(cell_ready, 1)

                depthwise(0, (0, 1))
                depthwise(0, (2, 3))
                chain.wait()
                dve.sem_inc(dw_done, 1)
                variances(n * CHUNKS)
                centre(n * CHUNKS)
                normalise_pixels(n * CHUNKS)
                STEPS = 36 + TILES + 2 + 3 + 1 + POINTS + POINTS - 1 + 3 + 1
                with dve.Fori(0, CHUNKS - 1) as c:
                    chain.enter(c, STEPS)
                    cells(c, c + n * CHUNKS, False)
                chain.leave(CHUNKS - 1)
                cells(CHUNKS - 1, n * CHUNKS + CHUNKS - 1, True)
                chain.wait()
                step(dve.tensor_reduce(far[:, 1:2], amax[:, :], AX_X, ALU.max))
                dve.tensor_scalar(far[:, 0:1], far[:, 1:2], REACH, None, ALU.is_gt).then_inc(far_ready, 1)
                barrier(dve, ph(n, PH_CELLS))

                with dve.Fori(0, CHUNKS) as i:
                    for s in range(ROWS):
                        yg = i * ROWS + (n * SIDE + s)
                        dve.wait_ge(cw_in[s % 4], i * 64 + (n * CHUNKS * 64 + 32 * (s // 4 + 1)))
                        dve.wait_ge(w_free, yg + 1)
                        cw = cw_ring[:, s % 4, :].rearrange("p (q h f) -> p q h f", q=WIN, h=2)[:, :, 0, :]
                        ins = dve.tensor_tensor(
                            w_ring[:, s % 2].rearrange("p (a q) t g -> p a q (t g)", q=WIN),
                            cw.unsqueeze(1).to_broadcast([P, WIN, WIN, P // 2]),
                            band.rearrange("p (a q) -> p a q", q=WIN).unsqueeze(3).to_broadcast([P, WIN, WIN, P // 2]), ALU.mult)
                        ins.then_inc(w_ready, 1)
                dve.wait_ge(flag_ps, n + 1)
                dve.tensor_scalar(farflag[:, :], ps[:, 6, 0:1], 0.5, None, ALU.is_gt).then_inc(flag_ready, 1)
                dve.wait_ge(flag_ready, n + 1)
                barrier(dve, ph(n, PH_SAMPLE))

                flag = dve.value_load(farflag[0:1, 0:1], min_val=0, max_val=1)
                with dve.If(flag > 0):
                    fc = Chain(dve, far_dve[n])

                    def fstep(ins):
                        fc.did(ins)
                        fc.wait()

                    INNER = 2 * 5 + 1 + 2 * POINTS - 1
                    fstep(dve.tensor_copy(f_pos[:, 0:POINTS], K[:, K_CX:K_CX + POINTS]))
                    fstep(dve.tensor_copy(f_pos[:, POINTS:2 * POINTS], K[:, K_CY:K_CY + POINTS]))
                    with dve.Fori(0, CHUNKS) as c:
                        outer = fc.base + fc.n + c * (TILES * (GROUPS * INNER + 1))
                        held(dve, far_load[n], c * 16 + 16)
                        with dve.Fori(0, TILES) as k:
                            with dve.Fori(0, GROUPS) as g:
                                it = c * KG + k * GROUPS + g
                                inner = Chain(dve, far_dve[n])
                                inner.base = outer + k * (GROUPS * INNER + 1) + g * INNER

                                def istep(ins):
                                    inner.did(ins)
                                    inner.wait()

                                io = iota[:, 0:SIDE].unsqueeze(1).to_broadcast([P, POINTS, SIDE])

                                def table(a):
                                    return f_om[:, a, :, bass.ds(k * GROUPS + g, 1)].to_broadcast([P, POINTS, SIDE])

                                for axis, dst in ((0, f_tx), (1, f_ty)):
                                    at = f_pos[:, axis * POINTS:(axis + 1) * POINTS].unsqueeze(2).to_broadcast([P, POINTS, SIDE])
                                    istep(dve.tensor_tensor(dst, at, io, ALU.subtract))
                                    istep(dve.tensor_tensor(dst, dst, table(axis), ALU.add))
                                    istep(dve.scalar_tensor_tensor(out=dst, in0=dst, scalar=-1.0, in1=dst, op0=ALU.mult, op1=ALU.max))
                                    istep(dve.tensor_scalar(dst, dst, -1.0, 1.0, ALU.mult, ALU.add))
                                    istep(dve.tensor_scalar(dst, dst, 0.0, None, ALU.max))
                                istep(dve.tensor_tensor(f_ty, f_ty, table(2), ALU.mult))
                                dve.wait_ge(far_mm[n], led(it * 8))
                                for q in range(POINTS):
                                    tyb = f_ty[:, q, :].unsqueeze(2).to_broadcast([P, SIDE, SIDE])
                                    txb = f_tx[:, q, :].unsqueeze(1).to_broadcast([P, SIDE, SIDE])
                                    istep(dve.tensor_tensor(f_wt if q == 0 else f_tmp, tyb, txb, ALU.mult))
                                    if q:
                                        istep(dve.tensor_tensor(f_wt, f_wt, f_tmp, ALU.add))
                                assert inner.n == INNER, inner.n
                                dve.sem_inc(far_step[n], 1)
                                for b in range(8):
                                    dve.wait_ge(far_tr[n], it * 8 + b + 1)
                                    dve.wait_ge(far_mm[n], led(it * 8 + b))
                                    dve.tensor_copy(f_col, ps[:, 4, :]).then_inc(far_cp[n], 1)
                                dve.wait_ge(far_mm[n], led(it * 8 + 8))
                                dve.wait_ge(far_out[n], led(it * 16))
                                dve.tensor_copy(f_out[0:GC, :], ps[0:GC, 5, 0:P]).then_inc(far_sb[n], 1)
                            dve.tensor_scalar(f_pos[:, POINTS:2 * POINTS], f_pos[:, POINTS:2 * POINTS], 2.0, None, ALU.add).then_inc(far_dve[n], 1)
                            dve.wait_ge(far_dve[n], outer + k * (GROUPS * INNER + 1) + (GROUPS * INNER + 1))
                barrier(dve, ph(n, PH_FAR))

                with dve.Fori(0, CHUNKS // 2) as i:
                    for par in range(2):
                        c = i * 2 + par
                        cg = c + n * CHUNKS
                        dve.wait_ge(o_ps, cg + 3)
                        dve.wait_ge(so_in[par], i * 32 + 32 * (n * CHUNKS // 2 + 1))
                        for o in range(CT):
                            ins = dve.scalar_tensor_tensor(out=x1_buf[:, par, o, :], in0=ps[:, 4 * par + o, :], scalar=chan_sb[:, o, 12:13],
                                                           in1=x1_buf[:, par, o, :], op0=ALU.add, op1=ALU.add)
                        ins.then_inc(x1_ready, 1)
                        dve.wait_ge(x1_ready, cg + 3)
                        for o in range(CT):
                            ins = dve.bn_stats(stats[:, o, bass.ds(c, 1), :].rearrange("p a s -> p (a s)"), x1_buf[:, par, o, :])
                        ins.then_inc(x1_counted, 1)
                dve.wait_ge(x1_counted, 2 + (n + 1) * CHUNKS)
                dve.wait_ge(x1_copied, 2 + (n + 1) * CHUNKS)
                group_norm(2 * n + 2, POW_IMAGE * n + 3 + CHUNKS)
                barrier(dve, ph(n, PH_OUT))

                def add_residual(slot, quad, ready, count):
                    dve.wait_ge(ready, count)
                    dve.wait_ge(res_in[slot], quad * 16 + 16)
                    dve.tensor_tensor(rbuf[:, slot, :], rbuf[:, slot, :], tbuf[:, slot, :], ALU.add).then_inc(job_added, 1)

                dve.wait_ge(g_free, n * 80 + 16 + 4)
                with dve.Fori(0, CHUNKS) as c:
                    chain.enter(c, 6)
                    quad = c + n * 16
                    for m in range(MT):
                        v = vsum[:, :, :]
                        step(dve.tensor_tensor(v, T[:, m, bass.ds(c * ROWS, ROWS), :], T[:, m, bass.ds(c * ROWS + 1, ROWS), :], ALU.add))
                        step(dve.tensor_tensor(v, v, T[:, m, bass.ds(c * ROWS + 2, ROWS), :], ALU.add))
                        hs = hsum[:, m, :].rearrange("p (y x) -> p y x", y=ROWS)
                        dve.wait_ge(pool_sb, led(c * 2 + n * 16))
                        step(dve.tensor_tensor(hs, v[:, :, 0:SIDE], v[:, :, 1:SIDE + 1], ALU.add))
                        dve.tensor_tensor(hs, hs, v[:, :, 2:SIDE + 2], ALU.add).then_inc(pooled, 1)
                        dve.wait_ge(pooled, c * 2 + (n * 16 + m + 1))
                    for m in range(MT):
                        add_residual(m, quad, g_free, c * 2 + (n * 80 + 16 + m + 5))
                    for m in range(MT):
                        add_residual(2 + m, quad, pool_sb, led(c * 2 + (n * 16 + m + 1)))
                chain.leave(CHUNKS)
                for first, group in ((8, 32), (12, 64)):
                    with dve.Fori(0, 4) as i:
                        for k in range(4):
                            add_residual(k, i + (n * 16 + first), g_free, i * 4 + (n * 80 + group + k + 5))
                barrier(dve, ph(n, PH_L1))


def _constant_table(np):
    k = np.zeros((P, K_COLS), np.float32)
    p = np.arange(P)
    k[:, K_MEAN:K_MEAN + P] = 1.0 / C
    k[:, K_GROUP:K_GROUP + P] = (p[:, None] // GROUPS == p[None, :] // GROUPS) / float(C // 32)
    k[:, K_EYE:K_EYE + P] = np.eye(P)
    k[:, K_BELOW:K_BELOW + P] = p[:, None] < p[None, :]
    k[:, K_ONE:K_ONE + P] = 1.0
    k[:, K_IOTA:K_IOTA + 2 * C] = np.arange(2 * C)
    x = p % SIDE
    k[:, K_BAND:K_BAND + SIDE] = np.abs(x[:, None] - np.arange(SIDE)[None, :]) <= 3
    k[:, K_INDEX:K_INDEX + 8] = np.arange(8)[None, :] * P + p[:, None]
    q = np.arange(POINTS)
    k[:, K_CX:K_CX + POINTS] = x[:, None] + (q // 3 - 1)[None, :]
    k[:, K_CY:K_CY + POINTS] = (p // SIDE)[:, None] + (q % 3 - 1)[None, :]
    k[:, K_SHIFT:K_SHIFT + NEAR] = 2 - np.arange(NEAR)
    k[:, K_POWER] = -0.5
    return k


def kernel(**inputs):
    import numpy as np
    import concourse.bacc as bacc
    from concourse.bass_utils import run_bass_kernel_spmd

    a = {name: np.asarray(v) for name, v in inputs.items()}

    def tiles(v):
        return v.reshape(CT, P, -1).transpose(1, 0, 2)

    off = a["L0_conv_off_w"].reshape(C, GROUPS, POINTS, 2)
    off_b = a["L0_conv_off_b"].reshape(GROUPS, POINTS, 2)

    def by_point(v):
        return v.swapaxes(-1, -2).reshape(*v.shape[:-2], GP)

    def taps_first(w):
        return w.reshape(w.shape[0], w.shape[1], TAPS).transpose(0, 2, 1).reshape(w.shape[0], -1)

    bns = np.stack([a["L1_conv_" + s] for s in ("bn31", "bn33", "bna1", "bna2")])
    arrays = {
        "x": a["x"].reshape(IMAGES, C, PIXELS),
        "chan": np.concatenate([tiles(a["L0_conv_dw_w"].reshape(C, TAPS)), tiles(a["L0_conv_dw_b"]),
                                tiles(a["L0_conv_ln_g"]), tiles(a["L0_conv_ln_b"]), tiles(a["L0_conv_out_b"])], axis=2),
        "in_w": a["L0_conv_in_w"],
        "in_b": a["L0_conv_in_b"],
        "wom": np.concatenate([by_point(off[..., 0]), by_point(off[..., 1]),
                               by_point(a["L0_conv_mask_w"].reshape(C, GROUPS, POINTS))], axis=1),
        "bom": np.concatenate([by_point(off_b[..., 0]), by_point(off_b[..., 1]),
                               by_point(a["L0_conv_mask_b"].reshape(GROUPS, POINTS))]),
        "out_w": a["L0_conv_out_w"],
        "w31": a["L1_conv_w31"].reshape(MID, C).T,
        "wmain_o": taps_first(a["L1_conv_w_main"]),
        "w33_o": taps_first(a["L1_conv_w33"]),
        "w1_o": a["L1_conv_w_1x1"].reshape(MID, C),
        "wa_o": a["L1_conv_wa1"].reshape(MID, C),
        "bn": bns.reshape(4, 4, MT, P).transpose(3, 0, 1, 2),
        "fuse": a["L1_conv_fuse_weight"],
        "score": a["L1_conv_c_score"],
        "score_col": a["L1_conv_c_score"].reshape(8, P).T,
        "consts": _constant_table(np),
    }
    nc = bacc.Bacc("TRN2", target_bir_lowering=False, num_devices=1)
    feeds, args = {}, []
    for name, v in arrays.items():
        feeds[f"in_{name}"] = np.ascontiguousarray(v)
        args.append(nc.dram_tensor(f"in_{name}", v.shape, mybir.dt.from_np(v.dtype), kind="ExternalInput").ap())
    out = nc.dram_tensor("out_0", [IMAGES * C * CHUNKS, PX], F32, kind="ExternalOutput").ap()
    conv_preact_program(nc, *args, out)
    r = run_bass_kernel_spmd(nc, [feeds], core_ids=[0])
    return r.results[0]["out_0"].reshape(IMAGES, C, SIDE, SIDE)
```

```python
from contextlib import ExitStack

import concourse.bass as bass
from concourse import mybir

ALU = mybir.AluOpType
ACT = mybir.ActivationFunctionType
AX_X = mybir.AxisListType.X
F32 = mybir.dt.float32
I32 = mybir.dt.int32

IMAGES, C, SIDE = 2, 512, 64
PIXELS = SIDE * SIDE
P = 128
CT = C // P
ROWS = 8
PX = ROWS * SIDE
CHUNKS = SIDE // ROWS
PAD = SIDE + 2
MAP = PAD * PAD
GROUPS, POINTS, GC = 16, 9, 32
GP = GROUPS * POINTS
OM = 3 * GP
TILES = PX // P
KG = TILES * GROUPS
REACH = 2.0
NEAR = 5
WIN = 8
CELL = WIN * WIN * GROUPS
MARGIN = WIN // 2
BEFORE = 3
PROWS = SIDE + 7
MID = C // 2
BRANCHES, MT = 4, MID // P
TAPS = 9
DW_PE = 2
NO_ROW = 4096
GN_EPS = LN_EPS = BN_EPS = 1e-5

K_MEAN, K_GROUP, K_EYE, K_BELOW, K_ONE = 0, P, 2 * P, 3 * P, 4 * P
K_IOTA = 5 * P
K_BAND = K_IOTA + SIDE
K_INDEX = K_BAND + SIDE
K_CX = K_INDEX + 8
K_CY = K_CX + POINTS
K_SHIFT = K_CY + POINTS
K_POWER = K_SHIFT + NEAR
K_COLS = K_POWER + 1
K_LONG = K_COLS

U_MAIN, U_33 = 0, TAPS * CT
U_ONE = U_33 + TAPS * MT
U_AVG = U_ONE + CT
UNITS = U_AVG + CT
GROUPS_W = UNITS // 2
MAIN, ONE, CONV3, AVG = range(BRANCHES)
V_RANK, V_SCALE, V_BIAS, V_TSCALE, V_TBIAS, NV = 0, 1, 2, 3, 4, 5

G_AVG, G_ONE, G_MAIN, G_31, G_33, G_IMAGE = 0, 16, 32, 40, 56, 64
QUADS = 12
POW_IMAGE = CHUNKS + 2


class Chain:

    def __init__(self, eng, sem):
        self.eng, self.sem, self.base, self.n = eng, sem, 0, 0

    def did(self, instruction):
        instruction.then_inc(self.sem, 1)
        self.n += 1

    def wait(self, back=0):
        self.eng.wait_ge(self.sem, self.base + self.n - back)

    def enter(self, i, per):
        self.start, self.per = self.base + self.n, per
        self.base, self.n = self.start + i * per, 0

    def leave(self, trips):
        assert self.n == self.per, (self.n, self.per)
        self.base, self.n = self.start + trips * self.per, 0


def conv_preact_program(nc, x, chan, in_w, in_b, wom, bom, out_w, w31, wmain_o, w33_o, w1_o, wa_o,
                        bn, fuse, score, score_col, consts, out):
    with ExitStack() as ctx:
        def sb(name, shape, dt=F32):
            return ctx.enter_context(nc.sbuf_tensor(name, shape, dt))

        def sem(name):
            return ctx.enter_context(nc.semaphore(name))

        def dram(name, shape):
            return nc.dram_tensor(name, shape, F32, kind="Internal").ap()

        proj_d = dram("proj_d", [PROWS, SIDE, C])
        cell_d = dram("cell_d", [PIXELS + 2 * MARGIN, CELL])
        om_d = dram("om_d", [CHUNKS, P, TILES * OM])
        samp_d = dram("samp_d", [C, PIXELS])
        mid_d = [dram(f"mid_d{n}", [C * CHUNKS, PX]) for n in range(IMAGES)]
        w_d = dram("w_d", [P, UNITS * MID])

        H = sb("H", [P, CT * MAP])
        H4 = H[:, :].rearrange("p (t y x) -> p t y x", t=CT, y=PAD)
        K = sb("K", [P, K_COLS])
        chan_sb = sb("chan_sb", [P, CT, 13])
        prm = sb("prm", [P, BRANCHES, MT, NV])
        rowidx = sb("rowidx", [P, BRANCHES * MT, IMAGES, CHUNKS], I32)
        jobidx = sb("jobidx", [P, 4, IMAGES], I32)
        t31p = sb("t31p", [P, MT, 2])
        stats = sb("stats", [P, CT, CHUNKS, 6])
        mv = sb("mv", [P, CT, 2])
        ag = sb("ag", [P, CT, 2])
        gs = sb("gs", [P, CT, 2])
        gtmp = sb("gtmp", [P, CT])
        nscale = sb("nscale", [P, CT])
        nbias = sb("nbias", [P, CT])
        amax = sb("amax", [P, CHUNKS])
        far = sb("far", [P, 2])
        farflag = sb("farflag", [P, 1], I32)
        spillflag = sb("spillflag", [P, BRANCHES], I32)
        small = sb("small", [P, 2, TILES * GROUPS])
        var = sb("var", [P, TILES])
        REGION = 33590
        R = sb("R", [P, REGION])

        def views(*shapes):
            at, made = 0, []
            for s in shapes:
                n = 1
                for d in s:
                    n *= d
                v = R[:, at:at + n]
                if len(s) > 1:
                    names = "abcdef"[:len(s)]
                    v = v.rearrange(f"p ({' '.join(names)}) -> p {' '.join(names)}",
                                    **{names[i]: s[i] for i in range(len(s))})
                made.append(v)
                at += n
            assert at <= REGION, at
            return made


        mean_w, group_w, eye, below_w, one_w = (K[:, k:k + P] for k in (K_MEAN, K_GROUP, K_EYE, K_BELOW, K_ONE))
        iota = K[:, K_IOTA:K_IOTA + SIDE]
        band = K[:, K_BAND:K_BAND + SIDE]
        jbias = K[:, K_SHIFT:K_SHIFT + NEAR]

        ps = ctx.enter_context(nc.psum_tensor("ps", [P, 8, 512], F32))
        DW_BANKS = (3, 0)

        def om_bank(k):
            return ps[:, 4 + k, 0:OM]

        phase_done = sem("phase_done")
        const_in, score_in, bn_in, small_w_in, main_w_in = (sem(s) for s in ("const_in", "score_in", "bn_in", "small_w_in", "main_w_in"))
        zero_ready, zero_out, border_ready = sem("zero_ready"), sem("zero_out"), sem("border_ready")
        x_in = [sem(f"x_in{t}") for t in range(CT)]
        dve_step, act_step, pool_step = sem("dve_step"), sem("act_step"), sem("pool_step")
        sel_ready, place_ready, onehot_ready, sig_ready = sem("sel_ready"), sem("place_ready"), sem("onehot_ready"), sem("sig_ready")
        pm_ready, prm_ps = sem("pm_ready"), sem("prm_ps")
        wp_ps, wp_sb = sem("wp_ps"), sem("wp_sb")
        wp_out = [sem(f"wp_out{k}") for k in range(4)]
        ag_ready, gstat_ps, nrm_ready, h_act, h_dve = sem("ag_ready"), sem("gstat_ps"), sem("nrm_ready"), sem("h_act"), sem("h_dve")
        passed = sem("passed")
        pow_asked, pow_done = sem("pow_asked"), sem("pow_done")
        l0w_in, hc_ready = sem("l0w_in"), sem("hc_ready")
        dw_done, y2_done, stat_ps, musq_done, ln_done, gelu_done = (sem(s) for s in ("dw_done", "y2_done", "stat_ps", "musq_done", "ln_done", "gelu_done"))
        om_ps, om_ready, tent_done, exp_done, cell_ready = (sem(s) for s in ("om_ps", "om_ready", "tent_done", "exp_done", "cell_ready"))
        cell_zero, diag_ready, rstd_ps = sem("cell_zero"), sem("diag_ready"), sem("rstd_ps")
        dwd_ready, dw_ps, dw_sb = sem("dwd_ready"), sem("dw_ps"), sem("dw_sb")
        cell_out, row_ready = sem("cell_out"), sem("row_ready")
        mask_ready, om_out = sem("mask_ready"), sem("om_out")
        xp_ps, xp_sb, xp_out = sem("xp_ps"), sem("xp_sb"), [sem("xp_out0"), sem("xp_out1")]
        p_in = [sem(f"p_in{k}") for k in range(8)]
        cw_in = [sem(f"cw_in{k}") for k in range(4)]
        w_ready, w_free, s_free = sem("w_ready"), sem("w_free"), sem("s_free")
        outw_in, flag_ps, flag_ready, far_ready = sem("outw_in"), sem("flag_ps"), sem("flag_ready"), sem("far_ready")
        x1_in = [sem("x1_in0"), sem("x1_in1")]
        o_ps, x1_ready, x1_copied, x1_counted = sem("o_ps"), sem("x1_ready"), sem("x1_copied"), sem("x1_counted")
        x1_out = [sem("x1_out0"), sem("x1_out1")]
        l1w_in, tzero = sem("l1w_in"), sem("tzero")
        g_ps, g_free, pooled, pool_sb, job_added = (sem(s) for s in ("g_ps", "g_free", "pooled", "pool_sb", "job_added"))
        res_in = [sem(f"res_in{k}") for k in range(4)]
        res_out = [sem(f"res_out{k}") for k in range(4)]
        class Spill:
            def __init__(self, b, n):
                self.ps, self.sb, self.added, self.idx, self.rows_in, self.rows_out = (
                    sem(f"spill_{what}{b}_{n}") for what in ("ps", "sb", "added", "idx", "rows_in", "rows_out"))

        SPILLS = (MAIN, CONV3)
        spills = {(b, n): Spill(b, n) for b in SPILLS for n in range(IMAGES)}
        far_load = [sem(f"far_load{n}") for n in range(IMAGES)]
        far_step = [sem(f"far_step{n}") for n in range(IMAGES)]
        far_w = [sem(f"far_w{n}") for n in range(IMAGES)]
        far_tr = [sem(f"far_tr{n}") for n in range(IMAGES)]
        far_cp = [sem(f"far_cp{n}") for n in range(IMAGES)]
        far_mm = [sem(f"far_mm{n}") for n in range(IMAGES)]
        far_sb = [sem(f"far_sb{n}") for n in range(IMAGES)]
        far_dve = [sem(f"far_dve{n}") for n in range(IMAGES)]
        far_out = [sem(f"far_out{n}") for n in range(IMAGES)]
        FAR_STEPS = CHUNKS * TILES * GROUPS
        redo_in, redo_ps, redo_x1, redo_copied, redo_counted, redo_out = far_load, far_mm, far_sb, far_tr, far_step, far_out

        def after_far(per_step, count):
            return per_step * FAR_STEPS + count

        (wmain_sb, w33_sb, w1_sb, wa_sb, onehot, sc_row, cmp_a, cmp_b, zeros, wstage, long_iota, prep) = views(
            [2, TAPS * C], [2, TAPS * MID], [2, C], [2, C], [BRANCHES, MT, MID], [2 * C], [2 * C], [2 * C],
            [2 * C], [4, 512], [2 * C], [400])
        (in_w_sb, hc, wom_sb, bom_sb, in_b_sb, y, ge, xp, om, tents, cell, prod, diag, dwd) = views(
            [CT, C], [CT, PX], [CT, OM], [OM], [C], [CT, PX], [CT, PX], [2, C], [3, POINTS, KG],
            [2, POINTS, NEAR, KG], [2, TILES * CELL], [2, NEAR, NEAR, KG], [PX], [DW_PE, TAPS, P])
        cell_acc = cell[:, 0, :].rearrange("p (e d f) -> p e d f", e=WIN, d=WIN)
        cell_row = cell[:, 1, :].rearrange("p (k f) -> p k f", k=TILES)
        (p_ring, cw_ring, w_ring, s_buf, out_w_sb, clear_of_cell_row, x1_buf) = views(
            [8, C], [4, CELL], [2, SIDE, 4, GROUPS], [2, CT, PX], [CT, C], [5200], [2, CT, PX])
        (f_om, f_tx, f_ty, f_wt, f_tmp, f_x, f_col, f_out, f_pos) = views(
            [3, POINTS, KG], [POINTS, SIDE], [POINTS, SIDE], [SIDE, SIDE], [SIDE, SIDE], [SIDE // 2, GC], [512], [P], [2 * POINTS])
        (T, lw, w31_sb, rbuf, tbuf, vsum, hsum) = views(
            [MT, PAD, PAD], [UNITS, MID], [CT, MID], [4, PX], [4, PX], [ROWS, PAD], [2, PX])

        s_col = prep[:, 0:8]
        rank = prep[:, 8:16]
        chosen = prep[:, 16:24]
        place = prep[:, 24:32]
        sig = prep[:, 32:40]
        bnp = prep[:, 40:72].rearrange("p (b k o) -> p b k o", b=4, k=4)
        bnsc = prep[:, 72:80].rearrange("p (b o) -> p b o", b=4)
        bnbi = prep[:, 80:88].rearrange("p (b o) -> p b o", b=4)
        fw = prep[:, 88:92]
        pm = prep[:, 92:132].rearrange("p (b o v) -> p b o v", b=BRANCHES, o=MT)
        base8 = prep[:, 132:140]

        def led(count):
            return count + 1

        def held(eng, semaphore, value):
            eng.wait_ge(semaphore, value)
            eng.sem_inc(passed, 1)

        def barrier(eng, k):
            eng.drain().then_inc(phase_done, 1)
            eng.wait_ge(phase_done, 5 * k)

        def x1_rows(n, c):
            return bass.AP(tensor=mid_d[n].tensor, offset=c * PX, ap=[[PIXELS, P], [P * PIXELS, CT], [1, PX]])

        PH_CELLS, PH_SAMPLE, PH_FAR, PH_OUT, PH_L1 = range(5)

        def ph(n, k):
            return 2 + 5 * n + k

        block = ctx.enter_context(nc.Block())

        @block.sync
        def _(sp):
            for semaphore in (*xp_out, cell_out, *far_out, om_out):
                sp.sem_inc(semaphore, 1)
            sp.dma_start(K[:, :], consts[:, 0:K_COLS]).then_inc(const_in, 16)
            sp.dma_start(long_iota, consts[:, K_LONG:K_LONG + 2 * C]).then_inc(const_in, 16)
            sp.dma_start(chan_sb[:, :, :], chan).then_inc(const_in, 16)
            sp.dma_start(sc_row, score.partition_broadcast(P)).then_inc(score_in, 16)
            sp.dma_start(s_col, score_col).then_inc(score_in, 16)
            sp.dma_start(bnp, bn).then_inc(bn_in, 16)
            sp.dma_start(fw, fuse.partition_broadcast(P)).then_inc(bn_in, 16)

            def load_x(n):
                for t in range(CT):
                    sp.dma_start(H4[:, t, 1:SIDE + 1, 1:SIDE + 1],
                                 x[n, t * P:(t + 1) * P, :].rearrange("p (y x) -> p y x", y=SIDE)).then_inc(x_in[t], 16)

            load_x(0)
            sp.dma_start(w1_sb, w1_o.rearrange("(o p) c -> p o c", p=P)).then_inc(small_w_in, 16)
            sp.dma_start(wa_sb, wa_o.rearrange("(o p) c -> p o c", p=P)).then_inc(small_w_in, 16)
            sp.dma_start(w33_sb, w33_o.rearrange("(o p) c -> p o c", p=P)).then_inc(small_w_in, 16)
            sp.dma_start(wmain_sb, wmain_o.rearrange("(o p) c -> p o c", p=P)).then_inc(main_w_in, 16)
            sp.wait_ge(zero_ready, 1)
            for r in (*range(BEFORE), *range(SIDE + BEFORE, PROWS)):
                sp.dma_start(proj_d[r], zeros[0:SIDE, 0:C]).then_inc(zero_out, 16)
            for r in (0, PIXELS):
                sp.dma_start(cell_d[r:r + 2 * MARGIN, :], zeros[0:2 * MARGIN, 0:CELL]).then_inc(zero_out, 16)
            for g in range(GROUPS_W):
                sp.wait_ge(wp_sb, g + 1)
                sp.dma_start(w_d[:, g * 512:(g + 1) * 512], wstage[:, g % 4, :]).then_inc(wp_out[g % 4], 16)
            for k in range(4):
                sp.wait_ge(wp_out[k], 16 * len(range(k, GROUPS_W, 4)))
            sp.wait_ge(zero_out, 16 * (PROWS - SIDE + 2))
            barrier(sp, 1)

            for n in range(IMAGES):
                sp.dma_start(in_w_sb, in_w.rearrange("(t p) o -> p t o", p=P)).then_inc(l0w_in, 16)
                sp.dma_start(wom_sb, wom.rearrange("(t p) o -> p t o", p=P)).then_inc(l0w_in, 16)
                sp.dma_start(bom_sb, bom.partition_broadcast(P)).then_inc(l0w_in, 16)
                sp.dma_start(in_b_sb[0:1, :], in_b.rearrange("(a c) -> a c", a=1)).then_inc(l0w_in, 16)

                def store_projection(c, cg):
                    for k in range(TILES):
                        sp.wait_ge(xp_sb, cg * TILES + (k + 1 + 2))
                        sp.dma_start(proj_d[bass.ds(c * ROWS + (BEFORE + 2 * k), 2)].rearrange("r x c -> (r x) c"),
                                     xp[:, k % 2, :]).then_inc(xp_out[k % 2], 16)

                def store_offsets(c, cg):
                    sp.wait_ge(mask_ready, cg + 1)
                    sp.dma_start(om_d[bass.ds(c, 1)].rearrange("a p f -> p (a f)"), om.rearrange("p a q f -> p (a q f)")).then_inc(om_out, 16)

                def store_cells(c, cg):
                    for k in range(TILES):
                        sp.wait_ge(row_ready, led(cg * TILES + (k + 1)))
                        for q in range(WIN):
                            dst = bass.AP(tensor=cell_d.tensor, offset=c * (PX * CELL) + ((k * P + q + 1) * CELL + q * P),
                                          ap=[[WIN * CELL, P // WIN], [CELL, WIN], [1, P]])
                            src = cell_row[q:P - WIN + q + 1:WIN, k, :].rearrange("p (e f) -> p e f", e=WIN)
                            sp.dma_start(dst, src).then_inc(cell_out, 16)

                def load_pair(m, slot):
                    sp.dma_start(p_ring[:, slot, :], proj_d[bass.ds(m, 2)].rearrange("y x c -> (y x) c")).then_inc(p_in[slot], 16)

                def load_weights(yy, s):
                    for h in range(2):
                        src = bass.AP(tensor=cell_d.tensor, offset=yy * (SIDE * CELL) + (MARGIN * CELL + h * (P // 2)),
                                      ap=[[CELL, SIDE], [1, CELL - P // 2]])
                        sp.dma_start(cw_ring[h * SIDE:(h + 1) * SIDE, s % 4, 0:CELL - P // 2], src).then_inc(cw_in[s % 4], 16)

                def feed(i, s, weights):
                    yy = i * ROWS + s
                    if weights:
                        sp.wait_ge(w_ready, yy + (n * SIDE + 1))
                        load_weights(yy, s)
                    sp.wait_ge(w_free, yy + (n * SIDE + 1))
                    load_pair(yy + 6, (s + 6) % 8)

                store_projection(0, n * CHUNKS)
                with sp.Fori(0, CHUNKS - 1) as c:
                    store_projection(c + 1, c + (n * CHUNKS + 1))
                    store_offsets(c, c + n * CHUNKS)
                    store_cells(c, c + n * CHUNKS)
                for par in range(2):
                    sp.wait_ge(xp_out[par], led(16 * (n + 1) * CHUNKS * TILES // 2))
                for m in range(6):
                    load_pair(m, m)
                sp.wait_ge(om_ready, led((n + 1) * CHUNKS))
                sp.wait_ge(cell_out, led(16 * WIN * TILES * ((n + 1) * CHUNKS - 1)))
                for s in range(4):
                    load_weights(s, s)
                store_offsets(CHUNKS - 1, (n + 1) * CHUNKS - 1)
                sp.wait_ge(om_out, led(16 * (n + 1) * CHUNKS))
                barrier(sp, ph(n, PH_CELLS))

                sp.dma_start(out_w_sb, out_w.rearrange("(t p) o -> p t o", p=P)).then_inc(outw_in, 16)
                store_cells(CHUNKS - 1, (n + 1) * CHUNKS - 1)
                for s in range(ROWS):
                    feed(0, s, s >= 4)
                sp.wait_ge(cell_out, led(16 * WIN * TILES * (n + 1) * CHUNKS))
                with sp.Fori(1, CHUNKS) as i:
                    for s in range(ROWS):
                        feed(i, s, True)
                barrier(sp, ph(n, PH_SAMPLE))

                sp.wait_ge(flag_ready, n + 1)
                flag = sp.value_load(farflag[0:1, 0:1], min_val=0, max_val=1)
                with sp.If(flag > 0):
                    with sp.Fori(0, CHUNKS) as c:
                        sp.wait_ge(far_sb[n], led(c * KG))
                        sp.dma_start(f_om.rearrange("p a q f -> p (a q f)"), om_d[bass.ds(c, 1)].rearrange("a p f -> p (a f)")).then_inc(far_load[n], 16)
                        with sp.Fori(0, TILES) as k:
                            with sp.Fori(0, GROUPS) as g:
                                it = c * KG + k * GROUPS + g
                                sp.wait_ge(far_sb[n], led(it))
                                src = bass.AP(tensor=proj_d.tensor, offset=g * GC + BEFORE * SIDE * C,
                                              ap=[[C, P], [2 * SIDE * C, SIDE // 2], [1, GC]])
                                sp.dma_start(f_x, src).then_inc(far_w[n], 16)
                                sp.wait_ge(far_sb[n], led(it + 1))
                                sp.dma_start(samp_d[bass.ds(g * GC, GC), bass.ds(c * PX + k * P, P)], f_out[0:GC, :]).then_inc(far_out[n], 16)
                                held(sp, far_out[n], led(it * 16 + 16))
                    sp.wait_ge(far_out[n], led(16 * CHUNKS * TILES * GROUPS))
                    with sp.Fori(0, CHUNKS) as c:
                        held(sp, redo_out[n], led(after_far(16, c * 16)))
                        held(sp, redo_copied[n], after_far(8, c))
                        held(sp, redo_counted[n], after_far(1, c))
                        sp.dma_start(s_buf[:, 0], samp_d[:, bass.ds(c * PX, PX)].rearrange("(t p) f -> p t f", p=P)).then_inc(redo_in[n], 16)
                        sp.dma_start(x1_buf[:, 0], x[n, :, bass.ds(c * PX, PX)].rearrange("(t p) f -> p t f", p=P)).then_inc(redo_in[n], 16)
                        held(sp, redo_x1[n], led(after_far(1, c + 1)))
                        sp.dma_start(x1_rows(n, c), x1_buf[:, 0]).then_inc(redo_out[n], 16)
                    sp.wait_ge(redo_out[n], led(after_far(16, 16 * CHUNKS)))
                barrier(sp, ph(n, PH_FAR))

                sp.dma_start(lw, w_d.rearrange("p (u f) -> p u f", u=UNITS)).then_inc(l1w_in, 16)
                sp.dma_start(w31_sb, w31.rearrange("(t p) o -> p t o", p=P)).then_inc(l1w_in, 16)
                barrier(sp, ph(n, PH_OUT))
                if n + 1 < IMAGES:
                    sp.wait_ge(g_free, n * G_IMAGE + G_33 + 4)
                    load_x(n + 1)
                barrier(sp, ph(n, PH_L1))

        @block.gpsimd
        def _(pool):
            chain = Chain(pool, pool_step)
            pool.memset(zeros, 0.0).then_inc(zero_ready, 1)
            for edge in (H4[:, :, 0, :], H4[:, :, PAD - 1, :], H4[:, :, 1:PAD - 1, 0], H4[:, :, 1:PAD - 1, PAD - 1]):
                pool.memset(edge, 0.0).then_inc(border_ready, 1)

            def inverse_root(v, width, k):
                pool.wait_ge(pow_asked, k)
                pool.tensor_tensor(v, v, K[:, K_POWER:K_POWER + 1].to_broadcast([P, width]), ALU.pow).then_inc(pow_done, 1)

            pool.wait_ge(const_in, 48)
            inverse_root(prep[:, 72:80], 8, 1)
            inverse_root(nscale[:, :], CT, 2)
            barrier(pool, 1)
            for n in range(IMAGES):
                if n:
                    inverse_root(nscale[:, :], CT, POW_IMAGE * n + 2)
                for t in range(DW_PE):
                    for tap in range(TAPS):
                        ins = pool.tensor_scalar(dwd[:, t, tap, :], eye, chan_sb[:, t, tap:tap + 1], None, ALU.mult)
                ins.then_inc(dwd_ready, 1)
                with pool.Fori(0, CHUNKS) as c:
                    inverse_root(var[:, :], TILES, c + (POW_IMAGE * n + 3))
                    held(pool, row_ready, led(c * TILES + n * (CHUNKS * TILES)))
                    pool.memset(cell_acc, 0.0).then_inc(cell_zero, 1)
                barrier(pool, ph(n, PH_CELLS))
                barrier(pool, ph(n, PH_SAMPLE))
                barrier(pool, ph(n, PH_FAR))
                for edge in (T[:, :, 0, :], T[:, :, PAD - 1, :], T[:, :, 1:PAD - 1, 0], T[:, :, 1:PAD - 1, PAD - 1]):
                    pool.memset(edge, 0.0).then_inc(tzero, 1)
                pool.memset(rbuf, 0.0).then_inc(tzero, 1)
                pool.wait_ge(tzero, 5 * (n + 1))
                inverse_root(nscale[:, :], CT, POW_IMAGE * n + 3 + CHUNKS)
                barrier(pool, ph(n, PH_OUT))

                def gather(bm, cc, slot):
                    chain.did(pool.tensor_copy(jobidx[:, slot, :], rowidx[:, bm, :, bass.ds(cc, 1)].rearrange("p n a -> p (n a)")))
                    held(pool, pool_step, chain.base + chain.n)
                    pool.indirect_dma_start(
                        out=rbuf[:, slot, :], out_offset=None, in_=mid_d[n],
                        in_offset=bass.IndirectOffsetOnAxis(ap=jobidx[:, slot, 0:1], axis=0),
                        bounds_check=C * CHUNKS - 1, oob_is_err=False).then_inc(res_in[slot], 16)

                def scatter(slot, job):
                    held(pool, job_added, job + 5)
                    pool.indirect_dma_start(
                        out=out, out_offset=bass.IndirectOffsetOnAxis(ap=jobidx[:, slot, n:n + 1], axis=0),
                        in_=rbuf[:, slot, :], in_offset=None,
                        bounds_check=IMAGES * C * CHUNKS - 1, oob_is_err=False).then_inc(res_out[slot], 16)

                def stream(kinds, chunk_of, trips, quad0):
                    def four_jobs(i, first):
                        quad = i + quad0
                        for k in range(4):
                            b, m = kinds[k]
                            if not first:
                                held(pool, res_out[k], quad * 16)
                            gather(b * MT + m, chunk_of(i, k), k)
                            if k >= 2:
                                scatter(k - 2, quad * 4 + k - 2)
                        scatter(2, quad * 4 + 2)
                        scatter(3, quad * 4 + 3)

                    peeled = 1 if quad0 == 0 else 0
                    if peeled:
                        four_jobs(0, True)
                    with pool.Fori(peeled, trips) as i:
                        chain.enter(i - peeled, 4)
                        four_jobs(i, False)
                    chain.leave(trips - peeled)

                def spill(b, quads):
                    for k in range(4):
                        pool.wait_ge(res_out[k], 16 * quads)
                    s_ = spills[b, n]
                    flag = pool.value_load(spillflag[0:1, b:b + 1], min_val=0, max_val=1)
                    with pool.If(flag > 0):
                        with pool.Fori(0, CHUNKS // 4) as i:
                            for k in range(4):
                                pool.tensor_copy(jobidx[:, k, :], rowidx[:, b * MT + 1, :, bass.ds(i * 4 + k, 1)].rearrange("p n a -> p (n a)")).then_inc(s_.idx, 1)
                            held(pool, s_.idx, i * 4 + 4)
                            for k in range(4):
                                pool.indirect_dma_start(
                                    out=rbuf[:, k, :], out_offset=None, in_=mid_d[n],
                                    in_offset=bass.IndirectOffsetOnAxis(ap=jobidx[:, k, 0:1], axis=0),
                                    bounds_check=C * CHUNKS - 1, oob_is_err=False).then_inc(s_.rows_in, 16)
                            held(pool, s_.added, led(i * 4 + 4))
                            for k in range(4):
                                pool.indirect_dma_start(
                                    out=out, out_offset=bass.IndirectOffsetOnAxis(ap=jobidx[:, k, n:n + 1], axis=0),
                                    in_=rbuf[:, k, :], in_offset=None,
                                    bounds_check=IMAGES * C * CHUNKS - 1, oob_is_err=False).then_inc(s_.rows_out, 16)
                            held(pool, s_.rows_out, i * 64 + 64)

                quads = n * QUADS
                stream([(ONE, 0), (ONE, 1), (AVG, 0), (AVG, 1)], lambda i, k: i, CHUNKS, quads)
                stream([(MAIN, 0)] * 4, lambda i, k: i * 4 + k, 2, quads + 8)
                spill(MAIN, quads + 10)
                stream([(CONV3, 0)] * 4, lambda i, k: i * 4 + k, 2, quads + 10)
                spill(CONV3, quads + 12)
                barrier(pool, ph(n, PH_L1))

        @block.scalar
        def _(act):
            chain = Chain(act, act_step)
            act.drain().then_inc(xp_sb, 2)
            for semaphore in (row_ready, pool_sb, *x1_out, *(s_.sb for s_ in spills.values())):
                act.sem_inc(semaphore, 1)
            act.drain().then_inc(s_free, 4)
            act.drain().then_inc(g_free, 4)
            act.drain().then_inc(x1_copied, 2)
            act.wait_ge(const_in, 48)
            act.wait_ge(score_in, 32)
            def normalise(k):
                act.wait_ge(nrm_ready, k)
                for t in range(2):
                    v = H4[:, t, 1:SIDE + 1, 1:SIDE + 1]
                    act.activation(v, v, ACT.Identity, bias=nbias[:, t:t + 1], scale=nscale[:, t:t + 1]).then_inc(h_act, 1)

            act.activation(sig, s_col, ACT.Sigmoid).then_inc(sig_ready, 1)
            for g in range(GROUPS_W):
                if g == 3 * GROUPS_W // 4:
                    normalise(1)
                act.wait_ge(wp_ps, g + 1)
                if g >= 4:
                    act.wait_ge(wp_out[g % 4], 16 * (g // 4))
                act.activation(wstage[:, g % 4, :], ps[:, g % 4, :], ACT.Copy).then_inc(wp_sb, 1)

            barrier(act, 1)
            for n in range(IMAGES):
                if n:
                    normalise(2 * n + 1)

                def head(c, cg):
                    act.wait_ge(ln_done, led(cg))
                    for t in range(DW_PE):
                        act.wait_ge(dw_ps, cg * DW_PE + (t + 1))
                        act.activation(y[:, t, :], ps[:, DW_BANKS[t], :], ACT.Identity, bias=chan_sb[:, t, 9:10]).then_inc(dw_sb, 1)
                    act.wait_ge(dw_sb, cg * DW_PE + DW_PE)
                    act.wait_ge(dw_done, cg + 1)
                    act.wait_ge(om_ps, led(TILES * cg))
                    act.activation(ge, y, ACT.Square).then_inc(y2_done, 1)
                    act.wait_ge(xp_ps, led(TILES * cg))
                    for t in range(CT):
                        ins = act.activation(hc[:, t, :].rearrange("p (y x) -> p y x", y=ROWS),
                                             H4[:, t, bass.ds(c * ROWS + 1, ROWS), 1:SIDE + 1], ACT.Copy)
                    ins.then_inc(hc_ready, 1)
                    act.wait_ge(stat_ps, cg + 1)
                    act.activation(diag, ps[:, 2, 0:PX], ACT.Square).then_inc(musq_done, 1)
                    for k in range(TILES):
                        act.wait_ge(xp_ps, led(TILES * cg + k + 1))
                        act.wait_ge(xp_out[k % 2], led(cg * (16 * TILES // 2) + 16 * (k // 2)))
                        act.activation(xp[:, k % 2, :], ps[:, k % 2, :], ACT.Copy).then_inc(xp_sb, 1)
                    act.wait_ge(ln_done, led(cg + 1))
                    for t in range(CT):
                        act.activation(ge[:, t, :], ge[:, t, :], ACT.Gelu, bias=chan_sb[:, t, 11:12], scale=chan_sb[:, t, 10:11]).then_inc(gelu_done, 1)

                def cells(c, cg, last):
                    act.wait_ge(om_ready, led(cg + 1))
                    act.wait_ge(cell_ready, led(cg))
                    act.activation(om[:, 2], om[:, 2], ACT.Exp).then_inc(exp_done, 1)
                    for j in range(NEAR):
                        ins = act.activation(
                            tents.rearrange("p a q j f -> p (a q) j f")[:, :, j, :],
                            om[:, 0:2].rearrange("p a q f -> p (a q) f"),
                            ACT.Abs, bias=jbias[:, j:j + 1])
                        chain.did(ins)
                    chain.wait()
                    act.activation(tents, tents, ACT.Relu, bias=jbias[:, 1:2], scale=-1.0).then_inc(tent_done, 1)
                    if not last:
                        head(c + 1, cg + 1)
                    act.wait_ge(cell_ready, led(cg + 1))
                    act.wait_ge(cell_out, led(cg * (16 * WIN * TILES)))
                    for k in range(TILES):
                        for h in range(2):
                            dst = cell_row[:, k].rearrange("p (e h t g) -> p e h t g", e=WIN, h=2, g=GROUPS)[:, :, h]
                            src = cell_acc.rearrange("p e (t h) (k g) -> p e t h k g", h=2, g=GROUPS)[:, :, :, h, k]
                            ins = act.activation(dst, src, ACT.Copy)
                        ins.then_inc(row_ready, 1)

                head(0, n * CHUNKS)
                with act.Fori(0, CHUNKS - 1) as c:
                    chain.enter(c, NEAR)
                    cells(c, c + n * CHUNKS, False)
                chain.leave(CHUNKS - 1)
                cells(CHUNKS - 1, n * CHUNKS + CHUNKS - 1, True)
                barrier(act, ph(n, PH_CELLS))

                def load_x_chunk(c, par, i):
                    held(act, x1_out[par], led((n * (CHUNKS // 2) + i) * 16))
                    held(act, x1_counted, c + (n * CHUNKS + 1))
                    act.dma_start(x1_buf[:, par], x[n, :, bass.ds(c * PX, PX)].rearrange("(t p) f -> p t f", p=P)).then_inc(x1_in[par], 16)

                def keep_x1(c, par):
                    act.wait_ge(x1_ready, c + (n * CHUNKS + 3))
                    for t in range(CT):
                        ins = act.activation(H4[:, t, bass.ds(c * ROWS + 1, ROWS), 1:SIDE + 1],
                                             x1_buf[:, par, t, :].rearrange("p (y x) -> p y x", y=ROWS), ACT.Copy)
                    ins.then_inc(x1_copied, 1)
                    held(act, x1_copied, c + (n * CHUNKS + 3))
                    act.dma_start(x1_rows(n, c), x1_buf[:, par]).then_inc(x1_out[par], 16)

                def collect(c, par, i, first):
                    cg = c + n * CHUNKS
                    load_x_chunk(c, par, i)
                    act.wait_ge(o_ps, cg + 1)
                    for pr in range(4):
                        act.wait_ge(w_free, cg * ROWS + 2 * pr + 4)
                        act.activation(s_buf[:, par, :, pr * P:(pr + 1) * P],
                                       ps[:, pr, :].rearrange("p (t f) -> p t f", t=CT), ACT.Copy).then_inc(s_free, 1)
                        if pr == 1 and not first:
                            keep_x1(c - 1, 1 - par)

                for par in range(2):
                    collect(par, par, 0, par == 0)
                with act.Fori(1, CHUNKS // 2) as i:
                    for par in range(2):
                        collect(i * 2 + par, par, i, False)
                keep_x1(CHUNKS - 1, 1)
                for par in range(2):
                    act.wait_ge(x1_out[par], led(16 * (n + 1) * CHUNKS // 2))
                barrier(act, ph(n, PH_SAMPLE))
                act.wait_ge(flag_ready, n + 1)
                flag = act.value_load(farflag[0:1, 0:1], min_val=0, max_val=1)
                with act.If(flag > 0):
                    with act.Fori(0, CHUNKS) as c:
                        act.wait_ge(redo_x1[n], led(after_far(1, c + 1)))
                        for t in range(CT):
                            ins = act.activation(H4[:, t, bass.ds(c * ROWS + 1, ROWS), 1:SIDE + 1],
                                                 x1_buf[:, 0, t, :].rearrange("p (y x) -> p y x", y=ROWS), ACT.Copy)
                        ins.then_inc(redo_copied[n], 1)
                barrier(act, ph(n, PH_FAR))

                normalise(2 * n + 2)
                barrier(act, ph(n, PH_OUT))

                act.wait_ge(tzero, 5 * (n + 1))
                gbase = n * G_IMAGE

                def to_map(prow, g0):
                    with act.Fori(0, CHUNKS // 2) as i:
                        for s in range(2):
                            for m in range(MT):
                                act.wait_ge(g_ps, i * 4 + (g0 + 2 * s + m + 1))
                                sc, bi = prow(m)
                                act.activation(T[:, m, bass.ds((i * 2 + s) * ROWS + 1, ROWS), 1:SIDE + 1],
                                               ps[:, 2 * s + m, :].rearrange("p (y x) -> p y x", y=ROWS),
                                               ACT.Identity, bias=bi, scale=sc).then_inc(g_free, 1)

                to_map(lambda m: (prm[:, AVG, m, V_TSCALE:V_TSCALE + 1], prm[:, AVG, m, V_TBIAS:V_TBIAS + 1]), gbase)
                jbase = n * 4 * QUADS

                def finish(b, m, bank, group, job, slot):
                    act.wait_ge(g_ps, group + 1)
                    act.wait_ge(job_added, job + 1)
                    act.activation(tbuf[:, slot, :], ps[:, bank, :], ACT.Identity, bias=prm[:, b, m, V_BIAS:V_BIAS + 1],
                                   scale=prm[:, b, m, V_SCALE:V_SCALE + 1]).then_inc(g_free, 1)

                with act.Fori(0, CHUNKS // 2) as i:
                    for s in range(2):
                        for m in range(MT):
                            finish(ONE, m, 2 * s + m, i * 4 + (gbase + 16 + 2 * s + m), i * 8 + (jbase + 4 * s + m), m)
                        for m in range(MT):
                            act.wait_ge(pooled, i * 4 + (n * 16 + 2 * s + m + 1))
                            act.wait_ge(job_added, i * 8 + (jbase + 4 * s + 2 + m + 1))
                            act.activation(tbuf[:, 2 + m, :], hsum[:, m, :], ACT.Identity, bias=prm[:, AVG, m, V_BIAS:V_BIAS + 1],
                                           scale=prm[:, AVG, m, V_SCALE:V_SCALE + 1]).then_inc(pool_sb, 1)
                def spill(b, jobs):
                    s_ = spills[b, n]
                    act.wait_ge(job_added, jobs + 4)
                    flag = act.value_load(spillflag[0:1, b:b + 1], min_val=0, max_val=1)
                    with act.If(flag > 0):
                        with act.Fori(0, CHUNKS // 4) as i:
                            for k in range(4):
                                act.wait_ge(s_.ps, i * 4 + (k + 1))
                                act.wait_ge(s_.added, led(i * 4))
                                act.activation(tbuf[:, k, :], ps[:, k, :], ACT.Identity, bias=prm[:, b, 1, V_BIAS:V_BIAS + 1],
                                               scale=prm[:, b, 1, V_SCALE:V_SCALE + 1]).then_inc(s_.sb, 1)
                        act.wait_ge(s_.added, led(CHUNKS))

                with act.Fori(0, CHUNKS // 4) as i:
                    for k in range(4):
                        finish(MAIN, 0, k, i * 4 + (gbase + G_MAIN + k), i * 4 + (jbase + 32 + k), k)
                spill(MAIN, jbase + 40)
                act.wait_ge(pooled, 2 * CHUNKS * (n + 1))
                to_map(lambda m: (t31p[:, m, 0:1], t31p[:, m, 1:2]), gbase + G_31)
                with act.Fori(0, CHUNKS // 4) as i:
                    for k in range(4):
                        finish(CONV3, 0, k, i * 4 + (gbase + G_33 + k), i * 4 + (jbase + 40 + k), k)
                spill(CONV3, jbase + 48)
                barrier(act, ph(n, PH_L1))

        @block.tensor
        def _(pe):
            pe.drain().then_inc(w_free, 2)
            for semaphore in (om_ps, xp_ps, *far_mm):
                pe.sem_inc(semaphore, 1)
            pe.drain().then_inc(o_ps, 2)
            pe.wait_ge(const_in, 48)
            pe.wait_ge(sel_ready, 1)
            pc = ps[:, 6, 0:8].rearrange("p (b o) -> p b o", b=BRANCHES)
            ch = chosen.rearrange("p (b o) -> p b o", b=BRANCHES)
            pe.matmul(pc[:, :, 0], below_w, ch[:, :, 0], start=True, stop=True)
            pe.matmul(pc[:, :, 1], below_w, ch[:, :, 1], start=True, stop=False)
            pe.matmul(pc[:, :, 1], one_w, ch[:, :, 0], start=False, stop=True)
            for o in range(MT):
                ins = pe.matmul(ps[:, 7, 0:BRANCHES], one_w, ch[:, :, o], start=(o == 0), stop=(o == MT - 1))
            ins.then_inc(place_ready, 1)
            def group_mean(k):
                pe.wait_ge(ag_ready, k)
                pe.matmul(ps[:, 7, 0:2 * CT], group_w, ag[:, :, :].rearrange("p t v -> p (t v)"), start=True, stop=True).then_inc(gstat_ps, 1)

            pe.wait_ge(onehot_ready, 8)
            units = []
            for tap in range(TAPS):
                for t in range(CT):
                    units.append((MAIN, wmain_sb, tap * C + t * P))
            for tap in range(TAPS):
                for t in range(MT):
                    units.append((CONV3, w33_sb, tap * MID + t * P))
            units += [(ONE, w1_sb, t * P) for t in range(CT)]
            units += [(AVG, wa_sb, t * P) for t in range(CT)]
            pe.wait_ge(main_w_in, 16)
            pe.wait_ge(small_w_in, 48)
            for g in range(GROUPS_W):
                if g == GROUPS_W // 2:
                    group_mean(1)
                if g >= 4:
                    pe.wait_ge(wp_sb, g - 3)
                for h in range(2):
                    b, w, at = units[2 * g + h]
                    for o in range(MT):
                        ins = pe.matmul(ps[:, g % 4, h * MID:(h + 1) * MID], w[:, o, at:at + P], onehot[:, b, o, :],
                                        start=(o == 0), stop=(o == MT - 1))
                ins.then_inc(wp_ps, 1)
            pe.wait_ge(pm_ready, 1)
            pp = ps[:, 5, 0:BRANCHES * MT * NV].rearrange("p (b m v) -> p b m v", b=BRANCHES, m=MT)
            for b in range(BRANCHES):
                for m in range(MT):
                    for o in range(MT):
                        ins = pe.matmul(pp[:, b, m, :], onehot[:, b, o, m * P:(m + 1) * P], pm[:, b, o, :],
                                        start=(o == 0), stop=(o == MT - 1))
            ins.then_inc(prm_ps, 1)

            barrier(pe, 1)
            for n in range(IMAGES):
                if n:
                    group_mean(2 * n + 1)
                pe.wait_ge(h_act, 2 * (2 * n + 1))
                pe.wait_ge(h_dve, 2 * (2 * n + 1))
                pe.wait_ge(l0w_in, 64 * (n + 1))

                pe.wait_ge(dwd_ready, n + 1)

                def depthwise(c, t):
                    for tap in range(TAPS):
                        ins = pe.matmul(ps[:, DW_BANKS[t], :], dwd[:, t, tap, :],
                                        H4[:, t, bass.ds(c * ROWS + tap // 3, ROWS), tap % 3:tap % 3 + SIDE],
                                        start=(tap == 0), stop=(tap == TAPS - 1))
                    ins.then_inc(dw_ps, 1)

                for t in range(DW_PE):
                    depthwise(0, t)

                def cells(c, cg, last):
                    pe.wait_ge(y2_done, cg + 1)
                    pe.wait_ge(ln_done, led(cg))
                    for bank, src in ((2, y), (3, ge)):
                        for t in range(CT):
                            ins = pe.matmul(ps[:, bank, 0:PX], mean_w, src[:, t, :], start=(t == 0), stop=(t == CT - 1))
                    ins.then_inc(stat_ps, 1)
                    pe.wait_ge(hc_ready, cg + 1)
                    for k in range(TILES):
                        pe.wait_ge(xp_sb, cg * TILES + (k + 1))
                        bank = ps[:, k % 2, :]
                        for t in range(CT):
                            pe.matmul(bank, hc[:, t, k * P:(k + 1) * P], in_w_sb[:, t, :],
                                      start=(t == 0), stop=False)
                        pe.matmul(bank, one_w[0:1, :], in_b_sb[0:1, :], start=False, stop=True).then_inc(xp_ps, 1)
                    pe.wait_ge(diag_ready, cg + 1)
                    pe.matmul(ps[:, 6, 0:PX], one_w, diag, start=True, stop=True).then_inc(rstd_ps, 1)
                    pe.wait_ge(gelu_done, cg * CT + CT)
                    pe.wait_ge(om_ready, led(cg))
                    for k in range(TILES):
                        for t in range(CT):
                            ins = pe.matmul(om_bank(k), ge[:, t, k * P:(k + 1) * P], wom_sb[:, t, :],
                                            start=(t == 0), stop=(t == CT - 1))
                        ins.then_inc(om_ps, 1)
                    if not last:
                        for t in range(DW_PE):
                            depthwise(c + 1, t)

                with pe.Fori(0, CHUNKS - 1) as c:
                    cells(c, c + n * CHUNKS, False)
                cells(CHUNKS - 1, n * CHUNKS + CHUNKS - 1, True)
                barrier(pe, ph(n, PH_CELLS))

                def project(sampled, done):
                    for o in range(CT):
                        for t in range(CT):
                            ins = pe.matmul(ps[:, 4 + o, :], out_w_sb[:, t, o * P:(o + 1) * P], sampled[:, t, :],
                                            start=(t == 0), stop=(t == CT - 1))
                    ins.then_inc(done, 1)

                pe.wait_ge(outw_in, 16 * (n + 1))
                with pe.Fori(0, CHUNKS // 2) as pair:
                    for par in range(2):
                        i = pair * 2 + par
                        for s in range(ROWS):
                            yg = i * ROWS + (n * SIDE + s)
                            pr, half = s // 2, s % 2
                            if half == 0:
                                pe.wait_ge(s_free, i * 4 + (n * 4 * CHUNKS + pr + 1))
                            pe.wait_ge(w_ready, yg + 5)
                            for t in range(4):
                                slot, uses = (s + 2 * t) % 8, (s + 2 * t) // 8 + 1
                                before = n * len(range(slot, SIDE + 6, 8))
                                pe.wait_ge(p_in[slot], i * 16 + 16 * (uses + before))
                            for ct in range(CT):
                                for t in range(4):
                                    slot = (s + 2 * t) % 8
                                    for j in range(4):
                                        g = ct * 4 + j
                                        ins = pe.matmul(ps[j * GC:(j + 1) * GC, pr, ct * P + half * SIDE:ct * P + (half + 1) * SIDE],
                                                        p_ring[:, slot, g * GC:(g + 1) * GC], w_ring[:, s % 2, :, t, g],
                                                        start=(t == 0), stop=(t == 3))
                            ins.then_inc(w_free, 1)
                        pe.wait_ge(s_free, i * 4 + (n * 4 * CHUNKS + 4 + 4))
                        pe.wait_ge(x1_ready, i + (n * CHUNKS + 2))
                        project(s_buf[:, par], o_ps)
                pe.wait_ge(far_ready, n + 1)
                pe.wait_ge(x1_ready, (n + 1) * CHUNKS + 2)
                pe.matmul(ps[:, 6, 0:1], one_w, far[:, 0:1], start=True, stop=True).then_inc(flag_ps, 1)
                barrier(pe, ph(n, PH_SAMPLE))

                pe.wait_ge(flag_ready, n + 1)
                flag = pe.value_load(farflag[0:1, 0:1], min_val=0, max_val=1)
                with pe.If(flag > 0):
                    with pe.Fori(0, CHUNKS * TILES * GROUPS) as it:
                        pe.wait_ge(far_w[n], it * 16 + 16)
                        pe.wait_ge(far_step[n], it + 1)
                        for b in range(8):
                            bb = it * 8 + b
                            pe.wait_ge(far_cp[n], led(bb))
                            for k in range(4):
                                ins = pe.transpose(ps[:, 4, k * P:(k + 1) * P],
                                                   f_wt[:, 2 * (4 * b + k):2 * (4 * b + k) + 2, :].rearrange("p y x -> p (y x)"), eye)
                            ins.then_inc(far_tr[n], 1)
                            pe.wait_ge(far_cp[n], led(bb + 1))
                            if b == 0:
                                pe.wait_ge(far_sb[n], led(it))
                            for k in range(4):
                                ins = pe.matmul(ps[0:GC, 5, 0:P], f_x[:, 4 * b + k, :], f_col[:, k * P:(k + 1) * P],
                                                start=(b == 0 and k == 0), stop=(b == 7 and k == 3))
                            ins.then_inc(far_mm[n], 1)
                    with pe.Fori(0, CHUNKS) as c:
                        pe.wait_ge(redo_in[n], c * 32 + (16 * CHUNKS + 32))
                        project(s_buf[:, 0], redo_ps[n])
                barrier(pe, ph(n, PH_FAR))

                group_mean(2 * n + 2)
                barrier(pe, ph(n, PH_OUT))

                pe.wait_ge(l1w_in, 32 * (n + 1))
                pe.wait_ge(h_act, 2 * (2 * n + 2))
                pe.wait_ge(h_dve, 2 * (2 * n + 2))
                gbase = n * G_IMAGE

                def products(g0, terms):
                    with pe.Fori(0, CHUNKS // 2) as i:
                        for s in range(2):
                            for m in range(MT):
                                pe.wait_ge(g_free, i * 4 + (g0 + 2 * s + m + 1))
                                row = i * (2 * ROWS) + s * ROWS
                                ts = terms(m)
                                for q, (w, src, t, ky, kx) in enumerate(ts):
                                    ins = pe.matmul(ps[:, 2 * s + m, :], w, src[:, t, bass.ds(row + ky, ROWS), kx:kx + SIDE],
                                                    start=(q == 0), stop=(q == len(ts) - 1))
                                ins.then_inc(g_ps, 1)

                def tile_products(first, terms):
                    with pe.Fori(0, CHUNKS // 4) as i:
                        for k in range(4):
                            pe.wait_ge(g_free, i * 4 + (first + k + 1))
                            row = i * (4 * ROWS) + k * ROWS
                            for q, (w, src, t, ky, kx) in enumerate(terms):
                                ins = pe.matmul(ps[:, k, :], w, src[:, t, bass.ds(row + ky, ROWS), kx:kx + SIDE],
                                                start=(q == 0), stop=(q == len(terms) - 1))
                            ins.then_inc(g_ps, 1)

                def spill(b, terms, groups):
                    s_ = spills[b, n]
                    pe.wait_ge(g_free, groups + 4)
                    flag = pe.value_load(spillflag[0:1, b:b + 1], min_val=0, max_val=1)
                    with pe.If(flag > 0):
                        with pe.Fori(0, CHUNKS // 4) as i:
                            for k in range(4):
                                pe.wait_ge(s_.sb, led(i * 4))
                                row = i * (4 * ROWS) + k * ROWS
                                for q, (w, src, t, ky, kx) in enumerate(terms):
                                    ins = pe.matmul(ps[:, k, :], w, src[:, t, bass.ds(row + ky, ROWS), kx:kx + SIDE],
                                                    start=(q == 0), stop=(q == len(terms) - 1))
                                ins.then_inc(s_.ps, 1)
                        pe.wait_ge(s_.sb, led(CHUNKS))

                def main_terms(m):
                    return [(lw[:, U_MAIN + tap * CT + t, m * P:(m + 1) * P], H4, t, tap // 3, tap % 3)
                            for tap in range(TAPS) for t in range(CT)]

                def conv3_terms(m):
                    return [(lw[:, U_33 + tap * MT + t, m * P:(m + 1) * P], T, t, tap // 3, tap % 3)
                            for tap in range(TAPS) for t in range(MT)]

                products(gbase + G_AVG, lambda m: [(lw[:, U_AVG + t, m * P:(m + 1) * P], H4, t, 1, 1) for t in range(CT)])
                products(gbase + G_ONE, lambda m: [(lw[:, U_ONE + t, m * P:(m + 1) * P], H4, t, 1, 1) for t in range(CT)])
                tile_products(gbase + G_MAIN, main_terms(0))
                spill(MAIN, main_terms(1), gbase + G_31)
                products(gbase + G_31, lambda m: [(w31_sb[:, t, m * P:(m + 1) * P], H4, t, 1, 1) for t in range(CT)])
                pe.wait_ge(g_free, gbase + G_33 + 4)
                tile_products(gbase + G_33, conv3_terms(0))
                spill(CONV3, conv3_terms(1), gbase + G_IMAGE)
                barrier(pe, ph(n, PH_L1))

        @block.vector
        def _(dve):
            chain = Chain(dve, dve_step)

            def step(ins):
                chain.did(ins)
                chain.wait()

            dve.drain().then_inc(w_ready, 4)
            for semaphore in (cell_ready, ln_done, om_ready, *far_cp, *far_sb, *(s_.added for s_ in spills.values())):
                dve.sem_inc(semaphore, 1)
            dve.drain().then_inc(x1_ready, 2)
            dve.drain().then_inc(x1_counted, 2)
            dve.drain().then_inc(job_added, 4)

            dve.wait_ge(const_in, 48)
            dve.wait_ge(score_in, 32)
            for t in range(8):
                step(dve.tensor_scalar(cmp_a, long_iota, K[:, K_INDEX + t:K_INDEX + t + 1], None, ALU.is_lt))
                step(dve.scalar_tensor_tensor(out=cmp_b, in0=sc_row, scalar=s_col[:, t:t + 1], in1=cmp_a, op0=ALU.is_equal, op1=ALU.mult))
                step(dve.scalar_tensor_tensor(out=cmp_a, in0=sc_row, scalar=s_col[:, t:t + 1], in1=cmp_b, op0=ALU.is_gt, op1=ALU.add))
                step(dve.tensor_reduce(rank[:, t:t + 1], cmp_a, AX_X, ALU.add))
            dve.tensor_scalar(chosen, rank, float(C), None, ALU.is_lt).then_inc(sel_ready, 1)
            dve.wait_ge(sel_ready, 1)
            dve.wait_ge(place_ready, 1)
            step(dve.tensor_copy(place, ps[:, 6, 0:8]))
            step(dve.tensor_scalar(spillflag[:, :], ps[:, 7, 0:BRANCHES], float(P), None, ALU.is_gt))
            for b in range(BRANCHES):
                for o in range(MT):
                    k = b * MT + o
                    dve.tensor_scalar(onehot[:, b, o, :], long_iota[:, 0:MID], place[:, k:k + 1], chosen[:, k:k + 1],
                                      ALU.is_equal, ALU.mult).then_inc(onehot_ready, 1)
            dve.wait_ge(bn_in, 32)
            dve.tensor_scalar(bnsc, bnp[:, :, 3, :], BN_EPS, None, ALU.add).then_inc(pow_asked, 1)
            dve.wait_ge(pow_done, 1)
            step(dve.tensor_tensor(bnsc, bnsc, bnp[:, :, 0, :], ALU.mult))
            step(dve.tensor_tensor(bnbi, bnsc, bnp[:, :, 2, :], ALU.mult))
            step(dve.tensor_tensor(bnbi, bnp[:, :, 1, :], bnbi, ALU.subtract))
            B31, B33, BA1, BA2 = range(4)
            step(dve.tensor_scalar(t31p[:, :, 0], bnsc[:, B31], fw[:, 2:3], None, ALU.mult))
            step(dve.tensor_copy(t31p[:, :, 1], bnbi[:, B31]))
            step(dve.memset(pm, 0.0))
            rk = rank.rearrange("p (b o) -> p b o", b=BRANCHES)
            dve.wait_ge(sig_ready, 1)
            sg = sig.rearrange("p (b o) -> p b o", b=BRANCHES)
            step(dve.tensor_scalar(pm[:, :, :, V_RANK], rk, -1.0, float(NO_ROW), ALU.mult, ALU.add))
            step(dve.tensor_scalar(pm[:, MAIN, :, V_SCALE], sg[:, MAIN], fw[:, 0:1], None, ALU.mult))
            step(dve.tensor_scalar(pm[:, ONE, :, V_SCALE], sg[:, ONE], fw[:, 1:2], None, ALU.mult))
            step(dve.tensor_tensor(pm[:, CONV3, :, V_SCALE], sg[:, CONV3], bnsc[:, B33], ALU.mult))
            step(dve.tensor_tensor(pm[:, CONV3, :, V_BIAS], sg[:, CONV3], bnbi[:, B33], ALU.mult))
            step(dve.scalar_tensor_tensor(out=pm[:, AVG, :, V_SCALE], in0=sg[:, AVG], scalar=1.0 / 9.0, in1=bnsc[:, BA2], op0=ALU.mult, op1=ALU.mult))
            step(dve.tensor_tensor(pm[:, AVG, :, V_BIAS], sg[:, AVG], bnbi[:, BA2], ALU.mult))
            step(dve.tensor_scalar(pm[:, AVG, :, V_TSCALE], bnsc[:, BA1], fw[:, 3:4], None, ALU.mult))
            dve.tensor_copy(pm[:, AVG, :, V_TBIAS], bnbi[:, BA1]).then_inc(pm_ready, 1)
            def slot_tables():
                dve.wait_ge(prm_ps, 1)
                step(dve.tensor_copy(prm[:, :, :, :], ps[:, 5, 0:BRANCHES * MT * NV].rearrange("p (b m v) -> p b m v", b=BRANCHES, m=MT)))
                step(dve.tensor_scalar(base8, prm[:, :, :, V_RANK].rearrange("p b m -> p (b m)"), -float(CHUNKS), float(NO_ROW * CHUNKS), ALU.mult, ALU.add))
                for n in range(IMAGES):
                    for c in range(CHUNKS):
                        ins = dve.tensor_scalar(rowidx[:, :, n, c], base8, float(n * C * CHUNKS + c), None, ALU.add)
                step(ins)

            def group_norm(k, kp):
                for t in range(CT):
                    chain.did(dve.bn_aggr(mv[:, t, :], stats[:, t].rearrange("p c s -> p (c s)")))
                chain.wait()
                step(dve.tensor_copy(ag[:, :, 0], mv[:, :, 0]))
                step(dve.tensor_tensor(ag[:, :, 1], mv[:, :, 0], mv[:, :, 0], ALU.mult))
                dve.tensor_tensor(ag[:, :, 1], ag[:, :, 1], mv[:, :, 1], ALU.add).then_inc(ag_ready, 1)
                dve.wait_ge(gstat_ps, k)
                step(dve.tensor_copy(gs[:, :, :], ps[:, 7, 0:2 * CT].rearrange("p (t v) -> p t v", v=2)))
                step(dve.tensor_tensor(gtmp[:, :], gs[:, :, 0], gs[:, :, 0], ALU.mult))
                step(dve.tensor_tensor(gtmp[:, :], gs[:, :, 1], gtmp[:, :], ALU.subtract))
                dve.tensor_scalar(nscale[:, :], gtmp[:, :], GN_EPS, None, ALU.add).then_inc(pow_asked, 1)
                dve.wait_ge(pow_done, kp)
                dve.scalar_tensor_tensor(out=nbias[:, :], in0=gs[:, :, 0], scalar=-1.0, in1=nscale[:, :], op0=ALU.mult, op1=ALU.mult).then_inc(nrm_ready, 1)
                dve.wait_ge(nrm_ready, k)
                for t in range(2, CT):
                    v = H4[:, t, 1:SIDE + 1, 1:SIDE + 1]
                    dve.tensor_scalar(v, v, nscale[:, t:t + 1], nbias[:, t:t + 1], ALU.mult, ALU.add).then_inc(h_dve, 1)

            def count_x(n):
                for t in range(CT):
                    dve.wait_ge(x_in[t], 16 * (n + 1))
                    for c in range(CHUNKS):
                        ins = dve.bn_stats(stats[:, t, c, :], H4[:, t, 1 + c * ROWS:1 + (c + 1) * ROWS, 1:SIDE + 1])
                step(ins)

            count_x(0)
            group_norm(1, 2)
            slot_tables()
            dve.wait_ge(border_ready, 4)
            barrier(dve, 1)

            for n in range(IMAGES):
                if n:
                    group_norm(2 * n + 1, POW_IMAGE * n + 2)
                dve.wait_ge(h_dve, 2 * (2 * n + 1))
                dve.wait_ge(h_act, 2 * (2 * n + 1))
                dve.wait_ge(l0w_in, 64 * (n + 1))

                def depthwise(c):
                    for tap in range(TAPS):
                        for t in range(DW_PE, CT):
                            src = H4[:, t, bass.ds(c * ROWS + tap // 3, ROWS), tap % 3:tap % 3 + SIDE]
                            dst = y[:, t, :].rearrange("p (y x) -> p y x", y=ROWS)
                            w = chan_sb[:, t, tap:tap + 1]
                            if tap == 0:
                                ins = dve.tensor_scalar(dst, src, w, chan_sb[:, t, 9:10], ALU.mult, ALU.add)
                            else:
                                chain.wait(CT - DW_PE - 1)
                                ins = dve.scalar_tensor_tensor(out=dst, in0=src, scalar=w, in1=dst, op0=ALU.mult, op1=ALU.add)
                            chain.did(ins)

                diag2, eye2 = diag.rearrange("p (k f) -> p k f", k=TILES), eye.unsqueeze(1).to_broadcast([P, TILES, P])

                def variances(cg):
                    dve.wait_ge(stat_ps, cg + 1)
                    dve.wait_ge(musq_done, cg + 1)
                    step(dve.tensor_tensor(diag, ps[:, 3, 0:PX], diag, ALU.subtract))
                    step(dve.tensor_tensor(diag2, diag2, eye2, ALU.mult))
                    step(dve.tensor_reduce(var[:, :], diag2, AX_X, ALU.add))
                    dve.tensor_scalar(var[:, :], var[:, :], LN_EPS, None, ALU.add).then_inc(pow_asked, 1)

                def centre(cg):
                    dve.wait_ge(pow_done, cg + (2 * n + 3))
                    dve.tensor_tensor(diag2, var[:, :].unsqueeze(2).to_broadcast([P, TILES, P]), eye2, ALU.mult).then_inc(diag_ready, 1)
                    step(dve.tensor_tensor(ge, y, ps[:, 2, 0:PX].unsqueeze(1).to_broadcast([P, CT, PX]), ALU.subtract))

                def normalise_pixels(cg):
                    dve.wait_ge(rstd_ps, cg + 1)
                    dve.tensor_tensor(ge, ge, ps[:, 6, 0:PX].unsqueeze(1).to_broadcast([P, CT, PX]), ALU.mult).then_inc(ln_done, 1)

                def cells(c, cg, last):
                    dve.wait_ge(om_out, led(cg * 16))
                    for k in range(TILES):
                        dve.wait_ge(om_ps, led(cg * TILES + k + 1))
                        chain.did(dve.tensor_tensor(
                            om.rearrange("p a q (k g) -> p (a q) k g", k=TILES)[:, :, k, :],
                            om_bank(k).rearrange("p (a g) -> p a g", g=GROUPS), bom_sb.rearrange("p (a g) -> p a g", g=GROUPS), ALU.add))
                    chain.wait()
                    logits, by_group = om[:, 2], om[:, 2].rearrange("p q f -> p f q")
                    sm, sr = small[:, 0, :], small[:, 1, :]
                    smb, srb = (v.unsqueeze(1).to_broadcast([P, POINTS, KG]) for v in (sm, sr))
                    step(dve.tensor_reduce(sm, by_group, AX_X, ALU.max))
                    chain.did(dve.tensor_reduce(amax[:, bass.ds(c, 1)], om[:, 0:2].rearrange("p a q f -> p (a q f)"), AX_X, ALU.max, apply_absolute_value=True))
                    dve.tensor_tensor(logits, logits, smb, ALU.subtract).then_inc(om_ready, 1)
                    if not last:
                        depthwise(c + 1)
                        chain.wait()
                        dve.sem_inc(dw_done, 1)
                    dve.wait_ge(exp_done, cg + 1)
                    step(dve.tensor_reduce(sm, by_group, AX_X, ALU.add))
                    step(dve.reciprocal(sr, sm))
                    dve.tensor_tensor(logits, logits, srb, ALU.mult).then_inc(mask_ready, 1)
                    dve.wait_ge(mask_ready, cg + 1)
                    dve.wait_ge(tent_done, cg + 1)
                    ty = tents[:, 1]
                    step(dve.tensor_tensor(ty, ty, logits.unsqueeze(2).to_broadcast([P, POINTS, NEAR, KG]), ALU.mult))
                    dve.wait_ge(cell_zero, cg + 1)

                    def product(q):
                        tx = tents[:, 0, q].unsqueeze(2).to_broadcast([P, NEAR, NEAR, KG])
                        u = tents[:, 1, q].unsqueeze(1).to_broadcast([P, NEAR, NEAR, KG])
                        chain.did(dve.tensor_tensor(prod[:, q % 2], tx, u, ALU.mult))

                    def sum_into(q):
                        gx, gy = q // 3, q % 3
                        acc = cell_acc[:, gx:gx + NEAR, gy:gy + NEAR, :]
                        return dve.tensor_tensor(acc, acc, prod[:, q % 2], ALU.add)

                    product(0)
                    for q in range(POINTS):
                        if not last and q == 4:
                            variances(cg + 1)
                        if not last and q == 5:
                            centre(cg + 1)
                        if not last and q == 6:
                            normalise_pixels(cg + 1)
                        if q + 1 < POINTS:
                            if q:
                                chain.wait()
                            product(q + 1)
                            chain.wait(1)
                            chain.did(sum_into(q))
                        else:
                            chain.wait()
                            sum_into(q).then_inc(cell_ready, 1)

                depthwise(0)
                chain.wait()
                dve.sem_inc(dw_done, 1)
                variances(n * CHUNKS)
                centre(n * CHUNKS)
                normalise_pixels(n * CHUNKS)
                STEPS = TAPS * (CT - DW_PE) + TILES + 2 + 2 + 1 + POINTS + POINTS - 1 + 3 + 1
                with dve.Fori(0, CHUNKS - 1) as c:
                    chain.enter(c, STEPS)
                    cells(c, c + n * CHUNKS, False)
                chain.leave(CHUNKS - 1)
                cells(CHUNKS - 1, n * CHUNKS + CHUNKS - 1, True)
                chain.wait()
                step(dve.tensor_reduce(far[:, 1:2], amax[:, :], AX_X, ALU.max))
                dve.tensor_scalar(far[:, 0:1], far[:, 1:2], REACH, None, ALU.is_gt).then_inc(far_ready, 1)
                barrier(dve, ph(n, PH_CELLS))

                def residual_out(c, buf, ready):
                    for o in range(CT):
                        ins = dve.scalar_tensor_tensor(out=buf[:, o, :], in0=ps[:, 4 + o, :], scalar=chan_sb[:, o, 12:13],
                                                       in1=buf[:, o, :], op0=ALU.add, op1=ALU.add)
                    ins.then_inc(ready, 1)

                def count(c, buf, counted):
                    for o in range(CT):
                        ins = dve.bn_stats(stats[:, o, bass.ds(c, 1), :].rearrange("p a s -> p (a s)"), buf[:, o, :])
                    ins.then_inc(counted, 1)

                def finish_chunk(c, par, i):
                    cg = c + n * CHUNKS
                    dve.wait_ge(o_ps, cg + 3)
                    dve.wait_ge(x1_in[par], i * 16 + 16 * (n * CHUNKS // 2 + 1))
                    residual_out(c, x1_buf[:, par], x1_ready)
                    dve.wait_ge(x1_ready, cg + 3)
                    count(c, x1_buf[:, par], x1_counted)

                def spread(i, s):
                    yg = i * ROWS + (n * SIDE + s)
                    dve.wait_ge(cw_in[s % 4], i * 64 + (n * CHUNKS * 64 + 32 * (s // 4 + 1)))
                    dve.wait_ge(w_free, yg + 1)
                    cw = cw_ring[:, s % 4, :].rearrange("p (q h f) -> p q h f", q=WIN, h=2)[:, :, 0, :]
                    ins = dve.tensor_tensor(
                        w_ring[:, s % 2].rearrange("p (a q) t g -> p a q (t g)", q=WIN),
                        cw.unsqueeze(1).to_broadcast([P, WIN, WIN, P // 2]),
                        band.rearrange("p (a q) -> p a q", q=WIN).unsqueeze(3).to_broadcast([P, WIN, WIN, P // 2]), ALU.mult)
                    ins.then_inc(w_ready, 1)

                def sample_chunk(c, par, i, first):
                    for s in range(ROWS):
                        if s == 2 and not first:
                            finish_chunk(c - 1, 1 - par, i - 1 + par)
                        spread(c, s)

                for par in range(2):
                    sample_chunk(par, par, 0, par == 0)
                with dve.Fori(1, CHUNKS // 2) as i:
                    for par in range(2):
                        sample_chunk(i * 2 + par, par, i, False)
                finish_chunk(CHUNKS - 1, 1, CHUNKS // 2 - 1)
                dve.wait_ge(flag_ps, n + 1)
                dve.tensor_scalar(farflag[:, :], ps[:, 6, 0:1], 0.5, None, ALU.is_gt).then_inc(flag_ready, 1)
                dve.wait_ge(flag_ready, n + 1)
                barrier(dve, ph(n, PH_SAMPLE))

                flag = dve.value_load(farflag[0:1, 0:1], min_val=0, max_val=1)
                with dve.If(flag > 0):
                    fc = Chain(dve, far_dve[n])

                    def fstep(ins):
                        fc.did(ins)
                        fc.wait()

                    INNER = 2 * 5 + 1 + 2 * POINTS - 1
                    fstep(dve.tensor_copy(f_pos[:, 0:POINTS], K[:, K_CX:K_CX + POINTS]))
                    fstep(dve.tensor_copy(f_pos[:, POINTS:2 * POINTS], K[:, K_CY:K_CY + POINTS]))
                    with dve.Fori(0, CHUNKS) as c:
                        outer = fc.base + fc.n + c * (TILES * (GROUPS * INNER + 1))
                        held(dve, far_load[n], c * 16 + 16)
                        with dve.Fori(0, TILES) as k:
                            with dve.Fori(0, GROUPS) as g:
                                it = c * KG + k * GROUPS + g
                                inner = Chain(dve, far_dve[n])
                                inner.base = outer + k * (GROUPS * INNER + 1) + g * INNER

                                def istep(ins):
                                    inner.did(ins)
                                    inner.wait()

                                io = iota[:, 0:SIDE].unsqueeze(1).to_broadcast([P, POINTS, SIDE])

                                def table(a):
                                    return f_om[:, a, :, bass.ds(k * GROUPS + g, 1)].to_broadcast([P, POINTS, SIDE])

                                for axis, dst in ((0, f_tx), (1, f_ty)):
                                    at = f_pos[:, axis * POINTS:(axis + 1) * POINTS].unsqueeze(2).to_broadcast([P, POINTS, SIDE])
                                    istep(dve.tensor_tensor(dst, at, io, ALU.subtract))
                                    istep(dve.tensor_tensor(dst, dst, table(axis), ALU.add))
                                    istep(dve.scalar_tensor_tensor(out=dst, in0=dst, scalar=-1.0, in1=dst, op0=ALU.mult, op1=ALU.max))
                                    istep(dve.tensor_scalar(dst, dst, -1.0, 1.0, ALU.mult, ALU.add))
                                    istep(dve.tensor_scalar(dst, dst, 0.0, None, ALU.max))
                                istep(dve.tensor_tensor(f_ty, f_ty, table(2), ALU.mult))
                                dve.wait_ge(far_mm[n], led(it * 8))
                                for q in range(POINTS):
                                    tyb = f_ty[:, q, :].unsqueeze(2).to_broadcast([P, SIDE, SIDE])
                                    txb = f_tx[:, q, :].unsqueeze(1).to_broadcast([P, SIDE, SIDE])
                                    istep(dve.tensor_tensor(f_wt if q == 0 else f_tmp, tyb, txb, ALU.mult))
                                    if q:
                                        istep(dve.tensor_tensor(f_wt, f_wt, f_tmp, ALU.add))
                                assert inner.n == INNER, inner.n
                                dve.sem_inc(far_step[n], 1)
                                for b in range(8):
                                    dve.wait_ge(far_tr[n], it * 8 + b + 1)
                                    dve.wait_ge(far_mm[n], led(it * 8 + b))
                                    dve.tensor_copy(f_col, ps[:, 4, :]).then_inc(far_cp[n], 1)
                                dve.wait_ge(far_mm[n], led(it * 8 + 8))
                                dve.wait_ge(far_out[n], led(it * 16))
                                dve.tensor_copy(f_out[0:GC, :], ps[0:GC, 5, 0:P]).then_inc(far_sb[n], 1)
                            dve.tensor_scalar(f_pos[:, POINTS:2 * POINTS], f_pos[:, POINTS:2 * POINTS], 2.0, None, ALU.add).then_inc(far_dve[n], 1)
                            dve.wait_ge(far_dve[n], outer + k * (GROUPS * INNER + 1) + (GROUPS * INNER + 1))
                    with dve.Fori(0, CHUNKS) as c:
                        dve.wait_ge(redo_ps[n], led(after_far(8, c + 1)))
                        residual_out(c, x1_buf[:, 0], redo_x1[n])
                        dve.wait_ge(redo_x1[n], led(after_far(1, c + 1)))
                        count(c, x1_buf[:, 0], redo_counted[n])
                barrier(dve, ph(n, PH_FAR))

                dve.wait_ge(x1_counted, 2 + (n + 1) * CHUNKS)
                dve.wait_ge(x1_copied, 2 + (n + 1) * CHUNKS)
                group_norm(2 * n + 2, POW_IMAGE * n + 3 + CHUNKS)
                barrier(dve, ph(n, PH_OUT))

                def add_residual(slot, quad, ready, count):
                    dve.wait_ge(ready, count)
                    dve.wait_ge(res_in[slot], quad * 16 + 16)
                    dve.tensor_tensor(rbuf[:, slot, :], rbuf[:, slot, :], tbuf[:, slot, :], ALU.add).then_inc(job_added, 1)

                dve.wait_ge(g_free, n * G_IMAGE + 16 + 4)
                with dve.Fori(0, CHUNKS) as c:
                    chain.enter(c, 6)
                    quad = c + n * QUADS
                    for m in range(MT):
                        v = vsum[:, :, :]
                        step(dve.tensor_tensor(v, T[:, m, bass.ds(c * ROWS, ROWS), :], T[:, m, bass.ds(c * ROWS + 1, ROWS), :], ALU.add))
                        step(dve.tensor_tensor(v, v, T[:, m, bass.ds(c * ROWS + 2, ROWS), :], ALU.add))
                        hs = hsum[:, m, :].rearrange("p (y x) -> p y x", y=ROWS)
                        dve.wait_ge(pool_sb, led(c * 2 + n * 16))
                        step(dve.tensor_tensor(hs, v[:, :, 0:SIDE], v[:, :, 1:SIDE + 1], ALU.add))
                        dve.tensor_tensor(hs, hs, v[:, :, 2:SIDE + 2], ALU.add).then_inc(pooled, 1)
                        dve.wait_ge(pooled, c * 2 + (n * 16 + m + 1))
                    for m in range(MT):
                        add_residual(m, quad, g_free, c * 2 + (n * G_IMAGE + 16 + m + 5))
                    for m in range(MT):
                        add_residual(2 + m, quad, pool_sb, led(c * 2 + (n * 16 + m + 1)))
                chain.leave(CHUNKS)
                for b, first, group in ((MAIN, 8, G_MAIN), (CONV3, 10, G_33)):
                    if b == CONV3 and n + 1 < IMAGES:
                        count_x(n + 1)
                    with dve.Fori(0, CHUNKS // 4) as i:
                        for k in range(4):
                            add_residual(k, i + (n * QUADS + first), g_free, i * 4 + (n * G_IMAGE + group + k + 5))
                    s_ = spills[b, n]
                    flag = dve.value_load(spillflag[0:1, b:b + 1], min_val=0, max_val=1)
                    with dve.If(flag > 0):
                        with dve.Fori(0, CHUNKS // 4) as i:
                            for k in range(4):
                                dve.wait_ge(s_.rows_in, i * 64 + 64)
                                dve.wait_ge(s_.sb, led(i * 4 + (k + 1)))
                                dve.tensor_tensor(rbuf[:, k, :], rbuf[:, k, :], tbuf[:, k, :], ALU.add).then_inc(s_.added, 1)
                barrier(dve, ph(n, PH_L1))


def _constant_table(np):
    k = np.zeros((P, K_LONG + 2 * C), np.float32)
    p = np.arange(P)
    k[:, K_MEAN:K_MEAN + P] = 1.0 / C
    k[:, K_GROUP:K_GROUP + P] = (p[:, None] // GROUPS == p[None, :] // GROUPS) / float(C // 32)
    k[:, K_EYE:K_EYE + P] = np.eye(P)
    k[:, K_BELOW:K_BELOW + P] = p[:, None] < p[None, :]
    k[:, K_ONE:K_ONE + P] = 1.0
    k[:, K_IOTA:K_IOTA + SIDE] = np.arange(SIDE)
    k[:, K_LONG:K_LONG + 2 * C] = np.arange(2 * C)
    x = p % SIDE
    k[:, K_BAND:K_BAND + SIDE] = np.abs(x[:, None] - np.arange(SIDE)[None, :]) <= 3
    k[:, K_INDEX:K_INDEX + 8] = np.arange(8)[None, :] * P + p[:, None]
    q = np.arange(POINTS)
    k[:, K_CX:K_CX + POINTS] = x[:, None] + (q // 3 - 1)[None, :]
    k[:, K_CY:K_CY + POINTS] = (p // SIDE)[:, None] + (q % 3 - 1)[None, :]
    k[:, K_SHIFT:K_SHIFT + NEAR] = 2 - np.arange(NEAR)
    k[:, K_POWER] = -0.5
    return k


def kernel(**inputs):
    import numpy as np
    import concourse.bacc as bacc
    from concourse.bass_utils import run_bass_kernel_spmd

    a = {name: np.asarray(v) for name, v in inputs.items()}

    def tiles(v):
        return v.reshape(CT, P, -1).transpose(1, 0, 2)

    off = a["L0_conv_off_w"].reshape(C, GROUPS, POINTS, 2)
    off_b = a["L0_conv_off_b"].reshape(GROUPS, POINTS, 2)

    def by_point(v):
        return v.swapaxes(-1, -2).reshape(*v.shape[:-2], GP)

    def taps_first(w):
        return w.reshape(w.shape[0], w.shape[1], TAPS).transpose(0, 2, 1).reshape(w.shape[0], -1)

    bns = np.stack([a["L1_conv_" + s] for s in ("bn31", "bn33", "bna1", "bna2")])
    arrays = {
        "x": a["x"].reshape(IMAGES, C, PIXELS),
        "chan": np.concatenate([tiles(a["L0_conv_dw_w"].reshape(C, TAPS)), tiles(a["L0_conv_dw_b"]),
                                tiles(a["L0_conv_ln_g"]), tiles(a["L0_conv_ln_b"]), tiles(a["L0_conv_out_b"])], axis=2),
        "in_w": a["L0_conv_in_w"],
        "in_b": a["L0_conv_in_b"],
        "wom": np.concatenate([by_point(off[..., 0]), by_point(off[..., 1]),
                               by_point(a["L0_conv_mask_w"].reshape(C, GROUPS, POINTS))], axis=1),
        "bom": np.concatenate([by_point(off_b[..., 0]), by_point(off_b[..., 1]),
                               by_point(a["L0_conv_mask_b"].reshape(GROUPS, POINTS))]),
        "out_w": a["L0_conv_out_w"],
        "w31": a["L1_conv_w31"].reshape(MID, C).T,
        "wmain_o": taps_first(a["L1_conv_w_main"]),
        "w33_o": taps_first(a["L1_conv_w33"]),
        "w1_o": a["L1_conv_w_1x1"].reshape(MID, C),
        "wa_o": a["L1_conv_wa1"].reshape(MID, C),
        "bn": bns.reshape(4, 4, MT, P).transpose(3, 0, 1, 2),
        "fuse": a["L1_conv_fuse_weight"],
        "score": a["L1_conv_c_score"],
        "score_col": a["L1_conv_c_score"].reshape(8, P).T,
        "consts": _constant_table(np),
    }
    nc = bacc.Bacc("TRN2", target_bir_lowering=False, num_devices=1)
    feeds, args = {}, []
    for name, v in arrays.items():
        feeds[f"in_{name}"] = np.ascontiguousarray(v)
        args.append(nc.dram_tensor(f"in_{name}", v.shape, mybir.dt.from_np(v.dtype), kind="ExternalInput").ap())
    out = nc.dram_tensor("out_0", [IMAGES * C * CHUNKS, PX], F32, kind="ExternalOutput").ap()
    conv_preact_program(nc, *args, out)
    r = run_bass_kernel_spmd(nc, [feeds], core_ids=[0])
    return r.results[0]["out_0"].reshape(IMAGES, C, SIDE, SIDE)
```
